# Optimizing a Trainium2 kernel written in Bass

```python
import numpy as np
import jax
import jax.numpy as jnp

def _softmax(x, axis=-1):
    return jax.nn.softmax(x, axis=axis)

def _gelu(x):
    return jax.nn.gelu(x, approximate=True)

def _silu(x):
    return jax.nn.silu(x)

def _sigmoid(x):
    return jax.nn.sigmoid(x)

def _layernorm(x, axis=-1, eps=1e-05):
    m = jnp.mean(x, axis=axis, keepdims=True)
    v = jnp.var(x, axis=axis, keepdims=True)
    return (x - m) / jnp.sqrt(v + eps)

def _scatter_add(tgt, idx, src, axis=0):
    return tgt.at[idx].add(src)

def _segment_sum(src, seg, n):
    return jax.ops.segment_sum(src, seg, n)
kernel_name = 'mk_gnn_preln_d1_gnn_r8_a14c38'

def setup_inputs(seed: int=0):
    np.random.seed(seed)
    _w = jnp.asarray

    def _rec_inputs():
        import jax
        import jax.numpy as jnp
        _gk = jax.random.key(seed)
        x = -0.000202 + 1 * jax.random.normal(jax.random.fold_in(_gk, 1), (6250, 128), jnp.float32)
        _s = jax.random.randint(jax.random.fold_in(_gk, 2), (50000,), 0, 6250, jnp.int32)
        _d = jax.random.randint(jax.random.fold_in(_gk, 3), (50000,), 0, 6250, jnp.int32)
        _loop = jnp.arange(6250, dtype=jnp.int32)
        src = jnp.concatenate([_s, _d, _loop])
        dst = jnp.concatenate([_d, _s, _loop])
        _o = jnp.argsort(dst, stable=True)
        src = src[_o]
        dst = dst[_o]
        edge_attr_128 = -8.16379e-05 + 0.999858 * jax.random.normal(jax.random.fold_in(_gk, 12), (106250, 128), jnp.float32)
        return (x, src, dst, edge_attr_128)
    x, src, dst, edge_attr_128 = _rec_inputs()

    def _L0_gnn_setup():
        import jax, jax.numpy as jnp
        import numpy as np
        N_NODES = 6250
        N_EDGES = 100000
        F_X = 128
        F_E = 128
        HIDDEN = 512
        F_OUT = 128
        key = jax.random.key(seed)
        k1, k2, k3, k4, k5, k6 = jax.random.split(key, 6)
        nodes = jax.random.normal(k1, (N_NODES, F_X), dtype=jnp.float32)
        edge_attr = jax.random.normal(k2, (N_EDGES, F_E), dtype=jnp.float32)
        senders = jax.random.randint(k3, (N_EDGES,), 0, N_NODES, dtype=jnp.int32)
        receivers = jax.random.randint(k4, (N_EDGES,), 0, N_NODES, dtype=jnp.int32)
        W1 = jax.random.normal(k5, (F_E + F_X, HIDDEN), dtype=jnp.float32) * (1.0 / np.sqrt(F_E + F_X))
        b1 = jnp.zeros((HIDDEN,), dtype=jnp.float32)
        W2 = jax.random.normal(k6, (HIDDEN, F_OUT), dtype=jnp.float32) * (1.0 / np.sqrt(HIDDEN))
        b2 = jnp.zeros((F_OUT,), dtype=jnp.float32)
        return {'nodes': nodes, 'edge_attr': edge_attr, 'senders': senders, 'receivers': receivers, 'W1': W1, 'b1': b1, 'W2': W2, 'b2': b2}
    _L0_gnn_all = _L0_gnn_setup()
    _L0_gnn_in = {k: v for k, v in _L0_gnn_all.items() if k in ('W1', 'b1', 'W2', 'b2')}
    del _L0_gnn_all
    return {'x': x, 'src': src, 'dst': dst, 'edge_attr_128': edge_attr_128, 'L0_gnn_W1': _L0_gnn_in['W1'], 'L0_gnn_b1': _L0_gnn_in['b1'], 'L0_gnn_W2': _L0_gnn_in['W2'], 'L0_gnn_b2': _L0_gnn_in['b2']}

def reference(x, src, dst, edge_attr_128, L0_gnn_W1, L0_gnn_b1, L0_gnn_W2, L0_gnn_b2):
    import jax
    import jax.numpy as jnp

    def _L0_gnn_ref(nodes, edge_attr, senders, receivers, W1, b1, W2, b2):
        import jax, jax.numpy as jnp
        import numpy as np
        N_NODES = 6250
        N_EDGES = 100000
        F_X = 128
        F_E = 128
        HIDDEN = 512
        F_OUT = 128
        agg = jax.ops.segment_sum(edge_attr, receivers, num_segments=N_NODES)
        x = jnp.concatenate([agg, nodes], axis=1)
        h = jax.nn.relu(x @ W1 + b1)
        return h @ W2 + b2
    h = jnp.maximum(_layernorm(x, axis=-1), 0.0)
    x = x + _L0_gnn_ref(h, edge_attr_128, src, dst, L0_gnn_W1, L0_gnn_b1, L0_gnn_W2, L0_gnn_b2)
    return x

_drawn_inputs = setup_inputs


def setup_inputs(seed=0):
    import zlib

    import numpy as np

    out = dict(_drawn_inputs(seed))
    spreads = {'L0_gnn_b1': (0.0, 0.1), 'L0_gnn_b2': (0.0, 0.1)}
    factors = {}
    for name, (base, spread) in spreads.items():
        noise = np.random.default_rng([zlib.crc32(name.encode()), seed]).standard_normal(out[name].shape)
        drawn = base * np.exp(spread * noise) if base else spread * noise
        out[name] = jnp.asarray(drawn.astype(out[name].dtype))
    for name, factor in factors.items():
        out[name] = (out[name] * factor).astype(out[name].dtype)
    return out
```

```python
from contextlib import ExitStack

import concourse.bass as bass
from concourse import mybir

P = 128
F32 = mybir.dt.float32
I32 = mybir.dt.int32
ALU = mybir.AluOpType
ACT = mybir.ActivationFunctionType
AX_X = mybir.AxisListType.X

G = 5
CHUNK = P * G
W = 48
SC = 7
BLOCK = 2 * P
LEAD = 3
WIDE = 512
PARTS = [(0, 2), (2, 2), (4, 3)]
BANK = [0, 1, 2, 3, 0, 1, 2, 3, 0, 1, 2, 0, 1, 2]
SINCE = [next(d for d in range(1, 15) if BANK[(i - d) % 14] == BANK[i]) for i in range(14)]


def graph_layer(nc, x, dst, edge_attr, W1, b1, W2, b2, out):
    N, F = x.shape
    E = edge_attr.shape[0]
    H = W1.shape[1]
    HT = H // P
    FULL = E // CHUNK
    REST = E - FULL * CHUNK
    KREST = REST // G
    NCH = FULL + 1
    NB = -(-N // BLOCK)
    NLAST = N - (NB - 1) * BLOCK
    STEPS = NB - 1
    CA, CB = P, NCH - P
    NWIDE = -(-N // WIDE)
    assert F == P and H == HT * P and HT == 4
    assert REST == KREST * G and 0 < KREST <= P and CHUNK % REST == 0
    assert STEPS % 2 == 0 and (STEPS - 1) * SC < NCH <= STEPS * SC and NLAST % 2 == 0
    LASTC = NCH - (STEPS - 1) * SC
    assert LASTC == 6

    def width(b):
        return NLAST // 2 if isinstance(b, int) and b == NB - 1 else P

    with ExitStack() as ctx:
        def sb(name, shape, dt=F32):
            return ctx.enter_context(nc.sbuf_tensor(name, shape, dt))

        def sem(name):
            return ctx.enter_context(nc.semaphore(name))

        edges = sb("edges", [P, 2 * SC, G * F])
        aggT = sb("aggT", [P, NWIDE * WIDE])
        hT = sb("hT", [P, NB * BLOCK])
        xs = sb("xs", [P, NB, 2 * F])
        dstA = sb("dstA", [P, CHUNK], I32)
        dstB = sb("dstB", [CB, CHUNK], I32)
        relA = sb("relA", [P, CHUNK])
        relB = sb("relB", [CB, CHUNK])
        relT = sb("relT", [P, STEPS * SC, G])
        colA = sb("colA", [P, 6])
        colB = sb("colB", [CB, 6])
        limit = sb("limit", [P, 2])
        limit_i = sb("limit_i", [P, 2], I32)
        base_row = sb("base_row", [1, STEPS * SC], I32)
        base_tab = sb("base_tab", [1, STEPS, 8], I32)
        over = sb("over", [1, 1])
        flag = sb("flag", [1, 1], I32)
        onehot = sb("onehot", [P, SC, G, W])
        iota_i = sb("iota_i", [P, WIDE], I32)
        iota = sb("iota", [P, WIDE])
        ident = sb("ident", [P, P])
        w1 = sb("w1", [P, 2, H])
        w2 = sb("w2", [P, HT, F])
        b1_row = sb("b1_row", [HT, P])
        b1_col = sb("b1_col", [P, HT])
        b2_all = sb("b2_all", [P, F])
        stats = sb("stats", [P, 2, 6])
        sums = sb("sums", [P, 2, 2, 2])
        diff = sb("diff", [P, 2, 2])
        diff2 = sb("diff2", [P, 2])
        mean = sb("mean", [P, 2, 2])
        vareps = sb("vareps", [P, 2])
        half = sb("half", [P, 2])
        rstd = sb("rstd", [P, 2, 2])
        xn = sb("xn", [P, 2, 2, F])
        hidden = [sb(f"hidden{i}", [P, HT, BLOCK]) for i in range(2)]
        outrow = sb("outrow", [P, 2, 2 * F])
        wide_hot = sb("wide_hot", [P, G, WIDE])
        wide_dst = sb("wide_dst", [P, G])

        bank = [ctx.enter_context(nc.psum_tensor(f"bank{i}", [P, 512], F32)) for i in range(8)]
        chunk_ps = bank[0:4]
        hid_ps = bank[4:6]
        tr_ps = bank[6]
        out_ps = bank[7]

        dst_landed = sem("dst_landed")
        x_first_landed = sem("x_first_landed")
        x_landed = [sem(f"x_landed{i}") for i in range(2)]
        x_last_landed = sem("x_last_landed")
        weights_landed = sem("weights_landed")
        edges_landed = [sem(f"edges_landed{i}") for i in range(2 * len(PARTS))]
        constants_ready = sem("constants_ready")
        agg_cleared = sem("agg_cleared")
        rel_ready = sem("rel_ready")
        rel_turned = sem("rel_turned")
        columns_turned = sem("columns_turned")
        banks_free = sem("banks_free")
        flag_ready = sem("flag_ready")
        onehot_ready = sem("onehot_ready")
        chunk_summed = sem("chunk_summed")
        agg_added = sem("agg_added")
        stats_done = sem("stats_done")
        stats_ready = sem("stats_ready")
        vareps_done = sem("vareps_done")
        rstd_ready = sem("rstd_ready")
        xn_ready = sem("xn_ready")
        residual_ready = sem("residual_ready")
        h_turned = sem("h_turned")
        hT_ready = sem("hT_ready")
        hidden_summed = sem("hidden_summed")
        hidden_ready = sem("hidden_ready")
        out_summed = sem("out_summed")
        out_added = sem("out_added")
        stored = [sem(f"stored{i}") for i in range(2)]
        vec_step = sem("vec_step")
        pool_step = sem("pool_step")
        wide_dst_ready = sem("wide_dst_ready")
        wide_rel_ready = sem("wide_rel_ready")
        wide_landed = sem("wide_landed")
        wide_hot_ready = sem("wide_hot_ready")
        wide_summed = sem("wide_summed")
        wide_added = sem("wide_added")

        chunks_v = edge_attr[0:FULL * CHUNK, :].rearrange("(c p g) f -> p c (g f)", p=P, g=G)
        rest_v = edge_attr[FULL * CHUNK:E, :].rearrange("(p g) f -> p (g f)", g=G)
        x_v = x[0:(NB - 1) * BLOCK, :].rearrange("(b p j) f -> p b (j f)", p=P, j=2)
        x_last_v = x[(NB - 1) * BLOCK:N, :].rearrange("(p j) f -> p (j f)", j=2)
        out_v = out[0:(NB - 1) * BLOCK, :].rearrange("(b p j) f -> p b (j f)", p=P, j=2)
        out_last_v = out[(NB - 1) * BLOCK:N, :].rearrange("(p j) f -> p (j f)", j=2)

        def at(t, i, n=1):
            return t[:, bass.ds(i, n)]

        def landed(eng, s, par, q, k):
            for i, (k0, n) in enumerate(PARTS):
                if k == k0:
                    eng.wait_ge(edges_landed[par * len(PARTS) + i], 16 * (q + 1))
            if isinstance(s, int) and s == STEPS - 1 and k == LASTC - 1:
                eng.wait_ge(edges_landed[par * len(PARTS) + 2], 16 * (q + 2))

        block = ctx.enter_context(nc.Block())

        @block.sync
        def _(sp):
            sp.dma_start(dstA[:, :], dst[0:P * CHUNK].rearrange("(c e) -> c e", e=CHUNK)).then_inc(dst_landed, 16)
            sp.dma_start(dstB[0:CB - 1, :],
                         dst[P * CHUNK:FULL * CHUNK].rearrange("(c e) -> c e", e=CHUNK)).then_inc(dst_landed, 16)
            rest = dst[FULL * CHUNK:E].rearrange("(a c e) -> a c e", a=1, c=1)
            sp.dma_start(dstB[CB - 1:CB, :].rearrange("a (c e) -> a c e", e=REST),
                         rest.to_broadcast([1, CHUNK // REST, REST])).then_inc(dst_landed, 16)

            def load(s, par, i, refill=True):
                k0, n = PARTS[i]
                if refill:
                    sp.wait_ge(chunk_summed, (s - 2) * SC + k0 + n)
                sp.dma_start(edges[:, par * SC + k0:par * SC + k0 + n, :],
                             chunks_v[:, bass.ds(s * SC + k0, n), :]
                             ).then_inc(edges_landed[par * len(PARTS) + i], 16)

            def load_x(b, par, q):
                if not isinstance(q, int) or q > 0:
                    sp.wait_ge(x_landed[par], 16 * q)
                sp.dma_start(xs[:, bass.ds(b, 1), :], x_v[:, bass.ds(b, 1), :]).then_inc(x_landed[par], 16)

            def store(n, par, b=None):
                b = n if b is None else b
                sp.wait_ge(out_added, n + 1)
                w = width(b)
                if w == P:
                    sp.dma_start(out_v[:, bass.ds(b, 1), :], outrow[:, par:par + 1, :]).then_inc(stored[par], 16)
                else:
                    sp.dma_start(out_last_v, outrow[0:w, par, :]).then_inc(stored[par], 16)

            for s in range(2):
                for i in range(len(PARTS)):
                    load(s, s, i, refill=False)
            for s in (2, 3):
                for i in range(len(PARTS)):
                    load(s, s % 2, i)
                load_x(s + 1, (s + 1) % 2, 0)
            with sp.Fori(0, 9) as m:
                for par in range(2):
                    s = 2 * m + 4 + par
                    load(s, par, 0)
                    load(s, par, 1)
                    load_x(s + 1, 1 - par, m + 1)
                    store(s - 4, par)
                    load(s, par, 2)
            s = STEPS - 2
            for i in range(len(PARTS)):
                load(s, 0, i)
            load_x(s + 1, 1, 10)
            store(s - 4, 0)
            s = STEPS - 1
            load(s, 1, 0)
            load(s, 1, 1)
            sp.wait_ge(chunk_summed, (s - 2) * SC + 6)
            sp.dma_start(edges[:, SC + 4, :], chunks_v[:, FULL - 1, :]).then_inc(edges_landed[5], 16)
            sp.wait_ge(edges_landed[5], 16 * 12)
            sp.dma_start(edges[0:KREST, SC + 5, :], rest_v).then_inc(edges_landed[5], 16)
            for b in range(s - 4, NB):
                store(b, b % 2)
            sp.wait_ge(stored[0], 16 * 13)
            sp.wait_ge(stored[1], 16 * 12)

            sp.wait_ge(flag_ready, 1)
            again = sp.value_load(flag[0:1, 0:1], min_val=0, max_val=1)
            with sp.If(again > 0):
                with sp.Fori(0, FULL) as c:
                    sp.wait_ge(wide_summed, c * NWIDE + 1)
                    sp.dma_start(edges[:, 0:1, :], chunks_v[:, bass.ds(c, 1), :]).then_inc(wide_landed, 16)
                sp.wait_ge(wide_summed, FULL * NWIDE + 1)
                sp.dma_start(edges[0:KREST, 0, :], rest_v).then_inc(wide_landed, 16)
                with sp.Fori(0, (NB - 1) // 2) as i:
                    store(NB + 2 * i, 1, 2 * i)
                    store(NB + 2 * i + 1, 0, 2 * i + 1)
                store(2 * NB - 1, 1, NB - 1)
                sp.wait_ge(stored[0], 16 * NB)
                sp.wait_ge(stored[1], 16 * NB)

        @block.gpsimd
        def _(pool):
            nc.gpsimd.memset(ident[:, :], 0.0).then_inc(pool_step, 1)
            nc.gpsimd.iota(iota_i[:, :], [[1, WIDE]], base=0, channel_multiplier=0).then_inc(pool_step, 1)
            nc.gpsimd.iota(limit_i[:, 0:1], [[0, 1]], base=-3 * BLOCK, channel_multiplier=BLOCK).then_inc(pool_step, 1)
            nc.gpsimd.iota(limit_i[:, 1:2], [[0, 1]], base=(P - 3) * BLOCK, channel_multiplier=BLOCK).then_inc(pool_step, 1)
            nc.gpsimd.memset(half[:, :], -0.5).then_inc(pool_step, 1)
            pool.wait_ge(pool_step, 5)
            nc.gpsimd.affine_select(out=ident[:, :], in_=ident[:, :], compare_op=ALU.not_equal, fill=1.0,
                                    base=0, pattern=[[-1, P]], channel_multiplier=1).then_inc(constants_ready, 1)
            nc.gpsimd.tensor_copy(limit[:, :], limit_i[:, :]).then_inc(constants_ready, 1)
            nc.gpsimd.tensor_copy(iota[:, :], iota_i[:, :]).then_inc(constants_ready, 1)
            nc.gpsimd.memset(aggT[:, :], 0.0).then_inc(agg_cleared, 1)
            pool.wait_ge(weights_landed, 16 * 4)

            def block_of(b, par, done):
                w = width(b)
                pool.wait_ge(stats_ready, b + 1)
                nc.gpsimd.tensor_tensor(diff2[0:w, :], diff[0:w, par, :], diff[0:w, par, :], ALU.mult)
                nc.gpsimd.tensor_scalar(mean[0:w, par, :], sums[0:w, par, :, 0], 0.5, 0.0, ALU.mult, ALU.add)
                nc.gpsimd.tensor_scalar(vareps[0:w, :], sums[0:w, par, :, 1], 4.0 / F, 4e-5, ALU.mult,
                                        ALU.add).then_inc(vareps_done, 1)
                pool.wait_ge(vareps_done, 2 * b + 1)
                nc.gpsimd.tensor_tensor(vareps[0:w, :], vareps[0:w, :], diff2[0:w, :], ALU.add).then_inc(vareps_done, 1)
                pool.wait_ge(vareps_done, 2 * b + 2)
                nc.gpsimd.tensor_tensor(rstd[0:w, par, :], vareps[0:w, :], half[0:w, :], ALU.pow).then_inc(rstd_ready, 1)
                pool.wait_ge(xn_ready, b + 1)
                r = xs[0:w, bass.ds(b, 1), :].rearrange("p b (j f) -> p (b j) f", j=2)
                nc.gpsimd.tensor_tensor(r, r, b2_all[0:w, :].unsqueeze(1).to_broadcast([w, 2, F]),
                                        ALU.add).then_inc(residual_ready, 1)

            with pool.Fori(0, (NB - 1) // 2) as i:
                block_of(2 * i, 0, None)
                block_of(2 * i + 1, 1, None)
            block_of(NB - 1, 0, None)

        @block.scalar
        def _(act):
            act.dma_start(xs[:, 0:3, :], x_v[:, 0:3, :]).then_inc(x_first_landed, 16)
            act.dma_start(b1_row[:, :], b1.rearrange("(t p) -> t p", p=P)).then_inc(weights_landed, 16)
            act.dma_start(b2_all[:, :], b2.partition_broadcast(P)).then_inc(weights_landed, 16)
            act.dma_start(w1[:, :, :], W1.rearrange("(t p) h -> p t h", p=P)).then_inc(weights_landed, 16)
            act.dma_start(w2[:, :, :], W2.rearrange("(t p) f -> p t f", p=P)).then_inc(weights_landed, 16)
            act.dma_start(xs[0:NLAST // 2, NB - 1, :], x_last_v).then_inc(x_last_landed, 16)

            def h_out(b):
                w = width(b)
                act.wait_ge(h_turned, b + 1)
                nc.scalar.activation(hT[:, bass.ds(b * BLOCK, 2 * w)], tr_ps[:, 0:2 * w], ACT.Relu,
                                     scale=2.0).then_inc(hT_ready, 1)

            def relu(n, par, b, first=False):
                w = width(b)
                for t in range(HT):
                    if t % 2 == 0:
                        act.wait_ge(hidden_summed, 2 * n + t // 2 + 1)
                    if t == 0 and not first:
                        act.wait_ge(out_summed, n - 1)
                    nc.scalar.activation(hidden[par][:, t, 0:2 * w],
                                         hid_ps[t // 2][:, (t % 2) * 2 * w:(t % 2 + 1) * 2 * w], ACT.Relu,
                                         bias=b1_col[:, t:t + 1]).then_inc(hidden_ready, 1)

            act.wait_ge(columns_turned, 1)
            nc.scalar.activation(b1_col[:, :], tr_ps[:, 0:HT], ACT.Copy).then_inc(hidden_ready, HT)
            act.wait_ge(hidden_ready, HT)
            h_out(0)
            h_out(1)
            relu(0, 0, 0, first=True)
            h_out(2)
            relu(1, 1, 1, first=True)
            with act.Fori(0, (STEPS - 4) // 2) as m:
                for par in range(2):
                    s = 2 * m + 3 + par
                    h_out(s)
                    relu(s - 1, par, s - 1)
            h_out(STEPS - 1)
            relu(STEPS - 2, 0, STEPS - 2)
            h_out(NB - 1)
            relu(NB - 2, 1, NB - 2)
            relu(NB - 1, 0, NB - 1)

            act.wait_ge(flag_ready, 1)
            again = act.value_load(flag[0:1, 0:1], min_val=0, max_val=1)
            with act.If(again > 0):
                with act.Fori(0, (NB - 1) // 2) as i:
                    relu(NB + 2 * i, 1, 2 * i)
                    relu(NB + 2 * i + 1, 0, 2 * i + 1)
                relu(2 * NB - 1, 1, NB - 1)

        @block.vector
        def _(dve):
            links = [0]

            def link(ins):
                links[0] += 1
                ins.then_inc(vec_step, 1)
                dve.wait_ge(vec_step, links[0])

            def build(c, slot):
                nc.vector.tensor_tensor(
                    onehot[:, slot, :, :], at(relT, c).rearrange("p c g -> p (c g)").unsqueeze(2).to_broadcast([P, G, W]),
                    iota[:, 0:W].unsqueeze(1).to_broadcast([P, G, W]), ALU.is_equal).then_inc(onehot_ready, 1)

            def statistics(b, par):
                w = width(b)
                for j in range(2):
                    ins = nc.vector.bn_stats(stats[0:w, j, :], xs[0:w, bass.ds(b, 1), j * F:(j + 1) * F]
                                             .rearrange("p b f -> p (b f)"))
                ins.then_inc(stats_done, 1)
                dve.wait_ge(stats_done, b + 1)
                nc.vector.tensor_tensor(sums[0:w, par, :, :], stats[0:w, :, 1:3], stats[0:w, :, 4:6], ALU.add)
                nc.vector.tensor_tensor(diff[0:w, par, :], stats[0:w, :, 1], stats[0:w, :, 4],
                                        ALU.subtract).then_inc(stats_ready, 1)

            def normalise(b, par, first=False):
                w = width(b)
                dve.wait_ge(rstd_ready, b + 1)
                if not first:
                    dve.wait_ge(h_turned, b - 1)
                for j in range(2):
                    ins = nc.vector.tensor_scalar(
                        xn[0:w, par, j, :], xs[0:w, bass.ds(b, 1), j * F:(j + 1) * F].rearrange("p b f -> p (b f)"),
                        mean[0:w, par, j:j + 1], rstd[0:w, par, j:j + 1], ALU.subtract, ALU.mult)
                ins.then_inc(xn_ready, 1)

            def add_chunk(c, base, slot, first=False):
                dve.wait_ge(chunk_summed, c + 1)
                if not first:
                    dve.wait_ge(agg_added, c)
                win = aggT[:, bass.ds(base, W)]
                nc.vector.tensor_tensor(win, chunk_ps[BANK[slot]][:, 0:W], win, ALU.add).then_inc(agg_added, 1)

            def finish(n, par, b, q, again=False):
                w = width(b)
                dve.wait_ge(out_summed, n + 1)
                if not again:
                    dve.wait_ge(residual_ready, n + 1)
                if not isinstance(q, int) or q > 0:
                    dve.wait_ge(stored[par], 16 * q)
                nc.vector.tensor_tensor(outrow[0:w, par, :], out_ps[0:w, 0:2 * F],
                                        xs[0:w, bass.ds(b, 1), :].rearrange("p b f -> p (b f)"),
                                        ALU.add).then_inc(out_added, 1)

            def step(s, par, q):
                last = isinstance(s, int) and s == STEPS - 1
                _, bases = nc.values_load_multi_w_load_instructions(
                    base_tab[0:1, bass.ds(s, 1), :].rearrange("a s k -> a (s k)"), engines=[dve.engine], min_val=0,
                    max_val=N - 1, skip_runtime_bounds_check_because="clamped when written")
                for k in range(LASTC if last else SC):
                    c = s * SC + k
                    if not last or k + LEAD < LASTC:
                        build(c + LEAD, (k + LEAD) % SC)
                    add_chunk(c, bases[k], par * SC + k, first=isinstance(c, int) and c == 0)
                    if k == 0 and (not isinstance(s, int) or s >= 2):
                        finish(s - 2, par, s - 2, q)
                    if k == 3:
                        if last:
                            dve.wait_ge(x_last_landed, 16)
                        elif not isinstance(s, int) or s >= 2:
                            dve.wait_ge(x_landed[1 - par], 16 * (q + 1))
                        statistics(s + 1, 1 - par)
                    if k == (4 if last else 5):
                        normalise(s + 1, 1 - par, first=isinstance(s, int) and s == 0)

            dve.wait_ge(dst_landed, 48)
            for d, col, rel in ((dstA, colA, relA), (dstB, colB, relB)):
                link(nc.vector.tensor_reduce(col[:, 0:1], d[:, :], AX_X, ALU.min))
                link(nc.vector.tensor_reduce(col[:, 1:2], d[:, :], AX_X, ALU.max))
                nc.vector.tensor_scalar(rel[:, :], d[:, :], col[:, 0:1], None, ALU.subtract).then_inc(rel_ready, 1)
            dve.wait_ge(constants_ready, 3)
            dve.wait_ge(rel_turned, 1)

            def turned(done):
                nc.vector.tensor_copy(relT[:, 0:P, 0:4].rearrange("p c g -> p g c"),
                                      chunk_ps[0][:, :].rearrange("p (g c) -> p g c", c=P))
                nc.vector.tensor_copy(relT[:, 0:P, 4], chunk_ps[1][:, 0:P])
                nc.vector.tensor_copy(relT[:, P:NCH, :].rearrange("p c g -> p g c"),
                                      chunk_ps[1][:, P:P + G * CB].rearrange("p (g c) -> p g c", c=CB)).then_inc(done, 1)

            turned(banks_free)
            for col, n, lim in ((colA, P, limit[:, 0:1]), (colB, CB, limit[0:CB, 1:2])):
                nc.vector.scalar_tensor_tensor(col[:, 2:3], col[:, 1:2], float(-(W - 1)), col[:, 0:1], ALU.add, ALU.subtract)
                link(nc.vector.scalar_tensor_tensor(col[:, 3:4], col[:, 0:1], float(-SC), lim, ALU.mult, ALU.add))
                nc.vector.tensor_tensor(col[:, 4:5], col[:, 2:3], col[:, 3:4], ALU.max).then_inc(rel_ready, 1)
            dve.wait_ge(columns_turned, 2)
            link(nc.vector.memset(base_row[:, :], 0))
            link(nc.vector.tensor_scalar(base_row[:, 0:NCH], hid_ps[0][0:1, 0:NCH], 0.0, float(N - 1), ALU.max, ALU.min))
            link(nc.vector.memset(base_tab[:, :, :], 0))
            nc.vector.tensor_copy(base_tab[:, :, 0:SC], base_row[:, :].rearrange("a (s k) -> a s k", k=SC))
            link(nc.vector.tensor_reduce(over[:, :], hid_ps[0][0:1, 256:256 + NCH], AX_X, ALU.max))
            nc.vector.tensor_scalar(flag[:, :], over[:, :], 0.0, None, ALU.is_gt).then_inc(flag_ready, 1)
            dve.wait_ge(flag_ready, 1)

            for c in range(LEAD):
                build(c, c)
            dve.wait_ge(x_first_landed, 16)
            statistics(0, 0)
            normalise(0, 0, first=True)
            dve.wait_ge(agg_cleared, 1)
            step(0, 0, None)
            step(1, 1, None)
            step(2, 0, 0)
            step(3, 1, 0)
            step(4, 0, 1)
            with dve.Fori(1, (STEPS - 4) // 2) as m:
                step(2 * m + 3, 1, m)
                step(2 * m + 4, 0, m + 1)
            step(STEPS - 1, 1, 10)
            for b in range(NB - 3, NB):
                finish(b, b % 2, b, b // 2)

            again = dve.value_load(flag[0:1, 0:1], min_val=0, max_val=1)
            with dve.If(again > 0):
                for col, rel, d in ((colA, relA, dstA), (colB, relB, dstB)):
                    hot = edges[0:rel.shape[0], 1, 0:CHUNK]
                    nc.vector.tensor_scalar(hot, rel[:, :], float(W), None, ALU.is_ge).then_inc(wide_dst_ready, 1)
                    nc.vector.tensor_scalar(col[:, 5:6], col[:, 0:1], 1.0, None, ALU.add).then_inc(wide_dst_ready, 1)
                    dve.wait_ge(wide_dst_ready, 2 if rel is relA else 4)
                    nc.vector.scalar_tensor_tensor(rel[:, :], rel[:, :], col[:, 5:6], hot, ALU.add,
                                                   ALU.mult).then_inc(wide_rel_ready, 1)
                    dve.wait_ge(wide_rel_ready, 1 if rel is relA else 2)
                dve.wait_ge(wide_summed, 1)
                turned(wide_added)

                def wide(c):
                    with dve.Fori(0, NWIDE) as j:
                        n = c * NWIDE + j
                        dve.wait_ge(wide_added, n + 1)
                        nc.vector.tensor_scalar(wide_dst[:, :], at(relT, c).rearrange("p c g -> p (c g)"),
                                                wide_base[:, bass.ds(j, 1)], None, ALU.subtract).then_inc(wide_dst_ready, 1)
                        dve.wait_ge(wide_dst_ready, 4 + n + 1)
                        nc.vector.tensor_tensor(wide_hot[:, :, :], wide_dst[:, :].unsqueeze(2).to_broadcast([P, G, WIDE]),
                                                iota[:, :].unsqueeze(1).to_broadcast([P, G, WIDE]),
                                                ALU.is_equal).then_inc(wide_hot_ready, 1)
                        dve.wait_ge(wide_summed, n + 2)
                        win = aggT[:, bass.ds(j * WIDE, WIDE)]
                        nc.vector.tensor_tensor(win, chunk_ps[0][:, :], win, ALU.add).then_inc(wide_added, 1)

                wide_base = xn[:, 0, 0, 0:NWIDE]
                for j in range(NWIDE):
                    nc.vector.memset(wide_base[:, j:j + 1], float(j * WIDE + 1)).then_inc(wide_rel_ready, 1)
                dve.wait_ge(wide_rel_ready, 2 + NWIDE)
                with dve.Fori(0, NCH) as c:
                    wide(c)
                with dve.Fori(0, (NB - 1) // 2) as i:
                    finish(NB + 2 * i, 1, 2 * i, i + NB // 2, again=True)
                    finish(NB + 2 * i + 1, 0, 2 * i + 1, i + NB // 2 + 1, again=True)
                finish(2 * NB - 1, 1, NB - 1, NB - 1, again=True)

        @block.tensor
        def _(pe):
            def turn_rel():
                for g in range(4):
                    nc.tensor.transpose(chunk_ps[0][:, g * P:(g + 1) * P], relA[:, g:CHUNK:G], ident[:, :])
                nc.tensor.transpose(chunk_ps[1][:, 0:P], relA[:, 4:CHUNK:G], ident[:, :])
                for g in range(G):
                    ins = nc.tensor.transpose(chunk_ps[1][:, P + g * CB:P + (g + 1) * CB], relB[:, g:CHUNK:G],
                                              ident[0:CB, 0:CB])
                return ins

            def sum_chunk(c, s, par, q, k):
                kp = KREST if isinstance(c, int) and c == NCH - 1 else P
                slot = par * SC + k
                landed(pe, s, par, q, k)
                pe.wait_ge(onehot_ready, c + 1)
                if not isinstance(c, int) or c >= SINCE[slot]:
                    pe.wait_ge(agg_added, c - SINCE[slot] + 1)
                for g in range(G):
                    ins = nc.tensor.matmul(chunk_ps[BANK[slot]][:, 0:W], edges[0:kp, slot, g * F:(g + 1) * F],
                                           onehot[0:kp, k, g, :], start=(g == 0), stop=(g == G - 1))
                ins.then_inc(chunk_summed, 1)

            def turn_x(b, par, first=False):
                w = width(b)
                pe.wait_ge(xn_ready, b + 1)
                if not first:
                    pe.wait_ge(hT_ready, b)
                for j in range(2):
                    ins = nc.tensor.transpose(tr_ps[:, j * w:(j + 1) * w], xn[0:w, par, j, :], ident[0:w, 0:w])
                ins.then_inc(h_turned, 1)

            def layer1(n, b):
                w = width(b)
                agg = aggT[:, bass.ds(b * BLOCK, 2 * w)].rearrange("f (p j) -> f j p", j=2)
                hrow = hT[:, bass.ds(b * BLOCK, 2 * w)].rearrange("f (j p) -> f j p", j=2)
                for t in range(HT):
                    if t % 2 == 0:
                        pe.wait_ge(hidden_ready, n * HT + t + 2)
                    o = hid_ps[t // 2][:, (t % 2) * 2 * w:(t % 2 + 1) * 2 * w].rearrange("f (j p) -> f j p", j=2)
                    nc.tensor.matmul(o, w1[:, 0, t * P:(t + 1) * P], agg, start=True, stop=False)
                    ins = nc.tensor.matmul(o, w1[:, 1, t * P:(t + 1) * P], hrow, start=False, stop=True)
                    if t % 2 == 1:
                        ins.then_inc(hidden_summed, 1)

            def layer2(n, par, b):
                w = width(b)
                if not isinstance(n, int) or n > 0:
                    pe.wait_ge(out_added, n)
                for j in range(2):
                    for t in range(HT):
                        if j == 0:
                            pe.wait_ge(hidden_ready, (n + 1) * HT + t + 1)
                        ins = nc.tensor.matmul(out_ps[0:w, j * F:(j + 1) * F], hidden[par][:, t, j * w:(j + 1) * w],
                                               w2[:, t, :], start=(t == 0), stop=(t == HT - 1))
                ins.then_inc(out_summed, 1)

            def step(s, par, q):
                for k in range(SC):
                    sum_chunk(s * SC + k, s, par, q, k)
                    if k == 0:
                        turn_x(s, par, first=isinstance(s, int) and s == 0)
                    if isinstance(s, int) and s == 0:
                        continue
                    if k == 4:
                        pe.wait_ge(agg_added, s * SC + 3)
                        pe.wait_ge(hT_ready, s)
                        layer1(s - 1, s - 1)
                    if k == 5:
                        layer2(s - 1, 1 - par, s - 1)

            pe.wait_ge(constants_ready, 1)
            pe.wait_ge(weights_landed, 64)
            nc.tensor.transpose(tr_ps[:, 0:HT], b1_row[:, :], ident[0:HT, 0:HT]).then_inc(columns_turned, 1)
            pe.wait_ge(rel_ready, 2)
            turn_rel().then_inc(rel_turned, 1)
            pe.wait_ge(rel_ready, 4)
            for i, col in ((0, 0), (256, 4)):
                nc.tensor.transpose(hid_ps[0][0:1, i:i + P], colA[:, col:col + 1], ident[:, :])
                ins = nc.tensor.transpose(hid_ps[0][0:1, i + P:i + NCH], colB[:, col:col + 1], ident[0:CB, 0:CB])
            ins.then_inc(columns_turned, 1)
            pe.wait_ge(banks_free, 1)
            pe.wait_ge(hidden_ready, HT)
            pe.wait_ge(flag_ready, 1)

            step(0, 0, 0)
            step(1, 1, 0)
            step(2, 0, 1)
            with pe.Fori(1, (STEPS - 2) // 2) as m:
                step(2 * m + 1, 1, m)
                step(2 * m + 2, 0, m + 1)
            s = STEPS - 1
            for k in range(LASTC):
                sum_chunk(s * SC + k, s, 1, 11, k)
                if k == 0:
                    turn_x(s, 1)
                if k == 3:
                    pe.wait_ge(agg_added, s * SC + 3)
                    pe.wait_ge(hT_ready, s)
                    layer1(s - 1, s - 1)
                if k == 4:
                    layer2(s - 1, 0, s - 1)
            turn_x(NB - 1, 0)
            pe.wait_ge(agg_added, NCH)
            layer1(NB - 2, NB - 2)
            pe.wait_ge(hT_ready, NB)
            layer1(NB - 1, NB - 1)
            layer2(NB - 2, 1, NB - 2)
            layer2(NB - 1, 0, NB - 1)

            again = pe.value_load(flag[0:1, 0:1], min_val=0, max_val=1)
            with pe.If(again > 0):
                pe.wait_ge(wide_rel_ready, 2)
                turn_rel().then_inc(wide_summed, 1)

                def wide(c, kp):
                    with pe.Fori(0, NWIDE) as j:
                        n = c * NWIDE + j
                        pe.wait_ge(wide_landed, 16 * (c + 1))
                        pe.wait_ge(wide_hot_ready, n + 1)
                        for g in range(G):
                            ins = nc.tensor.matmul(chunk_ps[0][:, :], edges[0:kp, 0, g * F:(g + 1) * F],
                                                   wide_hot[0:kp, g, :], start=(g == 0), stop=(g == G - 1))
                        ins.then_inc(wide_summed, 1)

                with pe.Fori(0, FULL) as c:
                    wide(c, P)
                wide(FULL, KREST)
                pe.wait_ge(wide_added, NCH * NWIDE + 1)
                with pe.Fori(0, (NB - 1) // 2) as i:
                    layer1(NB + 2 * i, 2 * i)
                    layer2(NB + 2 * i, 1, 2 * i)
                    layer1(NB + 2 * i + 1, 2 * i + 1)
                    layer2(NB + 2 * i + 1, 0, 2 * i + 1)
                layer1(2 * NB - 1, NB - 1)
                layer2(2 * NB - 1, 1, NB - 1)


_INS = ["x", "dst", "edge_attr_128", "L0_gnn_W1", "L0_gnn_b1", "L0_gnn_W2", "L0_gnn_b2"]


def kernel(**inputs):
    import numpy as _np
    import concourse.bacc as _bacc
    from concourse import mybir as _mybir
    from concourse.bass_utils import run_bass_kernel_spmd as _run

    nc = _bacc.Bacc("TRN2", target_bir_lowering=False, num_devices=1)
    arrays, args = {}, []
    for name in _INS:
        a = _np.ascontiguousarray(inputs[name])
        arrays[f"in_{name}"] = a
        args.append(nc.dram_tensor(f"in_{name}", a.shape, _mybir.dt.from_np(a.dtype), kind="ExternalInput").ap())
    out = nc.dram_tensor("out_rows", inputs["x"].shape, F32, kind="ExternalOutput").ap()
    graph_layer(nc, *args, out)
    r = _run(nc, [arrays], core_ids=[0])
    return r.results[0]["out_rows"]
```

```python
from contextlib import ExitStack

import concourse.bass as bass
from concourse import mybir

P = 128
F32 = mybir.dt.float32
F32R = mybir.dt.float32r
BF16 = mybir.dt.bfloat16
I32 = mybir.dt.int32
ALU = mybir.AluOpType
ACT = mybir.ActivationFunctionType
AX_X = mybir.AxisListType.X

G = 5
CHUNK = P * G
W = 48
SC = 7
BLOCK = 2 * P
LEAD = 6
WIDE = 512
PARTS = [(0, 2), (2, 2), (4, 3)]
BANK = [0, 1, 2, 3, 0, 1, 2, 3, 0, 1, 2, 0, 1, 2]
PLAIN = [0, 2, 4, 5]
HALVED = [1, 3, 5, 6]
POOLED = 6
SINCE = [next(d for d in range(1, 15) if BANK[(i - d) % 14] == BANK[i]) for i in range(14)]


def graph_layer(nc, x, dst, edge_attr, W1, b1, W2, b2, out):
    N, F = x.shape
    E = edge_attr.shape[0]
    H = W1.shape[1]
    HT = H // P
    FULL = E // CHUNK
    REST = E - FULL * CHUNK
    KREST = REST // G
    NCH = FULL + 1
    NB = -(-N // BLOCK)
    NLAST = N - (NB - 1) * BLOCK
    STEPS = NB - 1
    CA, CB = P, NCH - P
    NWIDE = -(-N // WIDE)
    assert F == P and H == HT * P and HT == 4
    assert REST == KREST * G and 0 < KREST <= P and CHUNK % REST == 0
    assert STEPS % 2 == 0 and (STEPS - 1) * SC < NCH <= STEPS * SC and NLAST % 2 == 0
    LASTC = NCH - (STEPS - 1) * SC
    assert LASTC == 6

    def width(b):
        return NLAST // 2 if isinstance(b, int) and b == NB - 1 else P

    with ExitStack() as ctx:
        def sb(name, shape, dt=F32):
            return ctx.enter_context(nc.sbuf_tensor(name, shape, dt))

        def sem(name):
            return ctx.enter_context(nc.semaphore(name))

        edges = sb("edges", [P, 2 * SC, G * F])
        aggT = sb("aggT", [P, NWIDE * WIDE])
        hT = sb("hT", [P, NB * BLOCK])
        xs = sb("xs", [P, NB, 2 * F])
        dstA = sb("dstA", [P, CHUNK], I32)
        dstB = sb("dstB", [CB, CHUNK], I32)
        relA = sb("relA", [P, CHUNK])
        relB = sb("relB", [CB, CHUNK])
        relT = sb("relT", [P, STEPS * SC, G])
        colA = sb("colA", [P, 6])
        colB = sb("colB", [CB, 6])
        limit = sb("limit", [P, 2])
        limit_i = sb("limit_i", [P, 2], I32)
        base_row = sb("base_row", [1, STEPS * SC], I32)
        base_tab = sb("base_tab", [1, STEPS, 8], I32)
        over = sb("over", [1, 1])
        flag = sb("flag", [1, 1], I32)
        onehot = sb("onehot", [P, len(PLAIN), G, W])
        onehot_h = sb("onehot_h", [P, len(HALVED), G, W], BF16)
        rem = sb("rem", [P, len(HALVED), G * F])
        low = sb("low", [P, len(HALVED), G * F], BF16)
        iota_i = sb("iota_i", [P, WIDE], I32)
        iota = sb("iota", [P, WIDE])
        ident = sb("ident", [P, P])
        w1 = sb("w1", [P, 2, H])
        w1_hi = sb("w1_hi", [P, H], F32R)
        w1_lo = sb("w1_lo", [P, H], F32R)
        agg_hi = sb("agg_hi", [P, 2, BLOCK], F32R)
        agg_lo = sb("agg_lo", [P, 2, BLOCK], F32R)
        w2 = sb("w2", [P, HT, F])
        b1_row = sb("b1_row", [HT, P])
        b1_col = sb("b1_col", [P, HT])
        b2_all = sb("b2_all", [P, F])
        stats = sb("stats", [P, 2, 6])
        sums = sb("sums", [P, 2, 2, 2])
        diff = sb("diff", [P, 2, 2])
        diff2 = sb("diff2", [P, 2])
        negmean = sb("negmean", [P, 2])
        shift = sb("shift", [P, 2, 2])
        vareps = sb("vareps", [P, 2])
        half = sb("half", [P, 2])
        rstd = sb("rstd", [P, 2, 2])
        xn = sb("xn", [P, 2, 2, F])
        hidden = [sb(f"hidden{i}", [P, HT, BLOCK]) for i in range(2)]
        outrow = sb("outrow", [P, 2, 2 * F])
        wide_hot = edges[:, 2:6, :].rearrange("p a b -> p (a b)").rearrange("p (g w) -> p g w", g=G)
        wide_dst = sb("wide_dst", [P, G])

        bank = [ctx.enter_context(nc.psum_tensor(f"bank{i}", [P, 512], F32)) for i in range(8)]
        chunk_ps = bank[0:4]
        hid_ps = bank[4:6]
        tr_ps = bank[6]
        out_ps = bank[7]

        dst_landed = sem("dst_landed")
        x_first_landed = sem("x_first_landed")
        x_landed = [sem(f"x_landed{i}") for i in range(2)]
        x_last_landed = sem("x_last_landed")
        weights_landed = sem("weights_landed")
        edges_landed = [sem(f"edges_landed{i}") for i in range(2 * len(PARTS))]
        constants_ready = sem("constants_ready")
        agg_cleared = sem("agg_cleared")
        rel_ready = sem("rel_ready")
        rel_turned = sem("rel_turned")
        columns_turned = sem("columns_turned")
        banks_free = sem("banks_free")
        flag_ready = sem("flag_ready")
        onehot_ready = sem("onehot_ready")
        chunk_summed = sem("chunk_summed")
        agg_added = sem("agg_added")
        stats_done = sem("stats_done")
        stats_ready = sem("stats_ready")
        vareps_done = sem("vareps_done")
        rstd_ready = sem("rstd_ready")
        xn_ready = sem("xn_ready")
        residual_ready = sem("residual_ready")
        w1_hi_ready = sem("w1_hi_ready")
        w1_ready = sem("w1_ready")
        rem_ready = sem("rem_ready")
        low_ready = sem("low_ready")
        pool_rem_ready = sem("pool_rem_ready")
        pool_low_ready = sem("pool_low_ready")
        agg_hi_ready = sem("agg_hi_ready")
        agg_lo_ready = sem("agg_lo_ready")
        h_turned = sem("h_turned")
        hT_ready = sem("hT_ready")
        hidden_summed = sem("hidden_summed")
        hidden_ready = sem("hidden_ready")
        out_summed = sem("out_summed")
        out_added = sem("out_added")
        stored = [sem(f"stored{i}") for i in range(2)]
        vec_step = sem("vec_step")
        pool_step = sem("pool_step")
        wide_dst_ready = sem("wide_dst_ready")
        wide_rel_ready = sem("wide_rel_ready")
        wide_landed = sem("wide_landed")
        wide_hot_ready = sem("wide_hot_ready")
        wide_summed = sem("wide_summed")
        wide_added = sem("wide_added")

        chunks_v = edge_attr[0:FULL * CHUNK, :].rearrange("(c p g) f -> p c (g f)", p=P, g=G)
        rest_v = edge_attr[FULL * CHUNK:E, :].rearrange("(p g) f -> p (g f)", g=G)
        x_v = x[0:(NB - 1) * BLOCK, :].rearrange("(b p j) f -> p b (j f)", p=P, j=2)
        x_last_v = x[(NB - 1) * BLOCK:N, :].rearrange("(p j) f -> p (j f)", j=2)
        out_v = out[0:(NB - 1) * BLOCK, :].rearrange("(b p j) f -> p b (j f)", p=P, j=2)
        out_last_v = out[(NB - 1) * BLOCK:N, :].rearrange("(p j) f -> p (j f)", j=2)

        def at(t, i, n=1):
            return t[:, bass.ds(i, n)]

        def landed(eng, s, par, q, k):
            for i, (k0, n) in enumerate(PARTS):
                if k == k0:
                    eng.wait_ge(edges_landed[par * len(PARTS) + i], 16 * (q + 1))
            if isinstance(s, int) and s == STEPS - 1 and k == LASTC - 1:
                eng.wait_ge(edges_landed[par * len(PARTS) + 2], 16 * (q + 2))

        def is_last(s):
            return isinstance(s, int) and s == STEPS - 1

        def plain(s, k):
            return k not in HALVED or (is_last(s) and k == LASTC - 1)

        def upper(t):
            n = t.shape[-1]
            return t.bitcast(BF16)[:, 1:2 * n:2]

        def take_apart(ops, eng, k, slot, n, rem_sem, low_sem):
            i = HALVED.index(k)
            e = edges[:, slot, :]
            ops.tensor_tensor(rem[:, i, :], e, upper(e), ALU.subtract).then_inc(rem_sem, 1)
            eng.wait_ge(rem_sem, n + 1)
            ops.tensor_tensor(low[:, i, :], rem[:, i, :], upper(rem[:, i, :]), ALU.subtract).then_inc(low_sem, 1)

        block = ctx.enter_context(nc.Block())

        @block.sync
        def _(sp):
            sp.dma_start(dstA[:, :], dst[0:P * CHUNK].rearrange("(c e) -> c e", e=CHUNK)).then_inc(dst_landed, 16)
            sp.dma_start(dstB[0:CB - 1, :],
                         dst[P * CHUNK:FULL * CHUNK].rearrange("(c e) -> c e", e=CHUNK)).then_inc(dst_landed, 16)
            rest = dst[FULL * CHUNK:E].rearrange("(a c e) -> a c e", a=1, c=1)
            sp.dma_start(dstB[CB - 1:CB, :].rearrange("a (c e) -> a c e", e=REST),
                         rest.to_broadcast([1, CHUNK // REST, REST])).then_inc(dst_landed, 16)

            def load(s, par, i, refill=True):
                k0, n = PARTS[i]
                if refill:
                    sp.wait_ge(chunk_summed, (s - 2) * SC + k0 + n)
                sp.dma_start(edges[:, par * SC + k0:par * SC + k0 + n, :],
                             chunks_v[:, bass.ds(s * SC + k0, n), :]
                             ).then_inc(edges_landed[par * len(PARTS) + i], 16)

            def load_x(b, par, q):
                if not isinstance(q, int) or q > 0:
                    sp.wait_ge(x_landed[par], 16 * q)
                sp.dma_start(xs[:, bass.ds(b, 1), :], x_v[:, bass.ds(b, 1), :]).then_inc(x_landed[par], 16)

            def store(n, par, b=None):
                b = n if b is None else b
                sp.wait_ge(out_added, n + 1)
                w = width(b)
                if w == P:
                    sp.dma_start(out_v[:, bass.ds(b, 1), :], outrow[:, par:par + 1, :]).then_inc(stored[par], 16)
                else:
                    sp.dma_start(out_last_v, outrow[0:w, par, :]).then_inc(stored[par], 16)

            for s in range(2):
                for i in range(len(PARTS)):
                    load(s, s, i, refill=False)
            for s in (2, 3):
                for i in range(len(PARTS)):
                    load(s, s % 2, i)
                load_x(s + 1, (s + 1) % 2, 0)
            with sp.Fori(0, 9) as m:
                for par in range(2):
                    s = 2 * m + 4 + par
                    load(s, par, 0)
                    load(s, par, 1)
                    load_x(s + 1, 1 - par, m + 1)
                    store(s - 4, par)
                    load(s, par, 2)
            s = STEPS - 2
            for i in range(len(PARTS)):
                load(s, 0, i)
            load_x(s + 1, 1, 10)
            store(s - 4, 0)
            s = STEPS - 1
            load(s, 1, 0)
            load(s, 1, 1)
            sp.wait_ge(chunk_summed, (s - 2) * SC + 6)
            sp.dma_start(edges[:, SC + 4, :], chunks_v[:, FULL - 1, :]).then_inc(edges_landed[5], 16)
            sp.wait_ge(edges_landed[5], 16 * 12)
            sp.dma_start(edges[0:KREST, SC + 5, :], rest_v).then_inc(edges_landed[5], 16)
            for b in range(s - 4, NB):
                store(b, b % 2)
            sp.wait_ge(stored[0], 16 * 13)
            sp.wait_ge(stored[1], 16 * 12)

            sp.wait_ge(flag_ready, 1)
            again = sp.value_load(flag[0:1, 0:1], min_val=0, max_val=1)
            with sp.If(again > 0):
                with sp.Fori(0, FULL) as c:
                    sp.wait_ge(wide_summed, c * NWIDE + 1)
                    sp.dma_start(edges[:, 0:1, :], chunks_v[:, bass.ds(c, 1), :]).then_inc(wide_landed, 16)
                sp.wait_ge(wide_summed, FULL * NWIDE + 1)
                sp.dma_start(edges[0:KREST, 0, :], rest_v).then_inc(wide_landed, 16)
                with sp.Fori(0, (NB - 1) // 2) as i:
                    store(NB + 2 * i, 1, 2 * i)
                    store(NB + 2 * i + 1, 0, 2 * i + 1)
                store(2 * NB - 1, 1, NB - 1)
                sp.wait_ge(stored[0], 16 * NB)
                sp.wait_ge(stored[1], 16 * NB)

        @block.gpsimd
        def _(pool):
            nc.gpsimd.memset(ident[:, :], 0.0).then_inc(pool_step, 1)
            nc.gpsimd.iota(iota_i[:, :], [[1, WIDE]], base=0, channel_multiplier=0).then_inc(pool_step, 1)
            nc.gpsimd.iota(limit_i[:, 0:1], [[0, 1]], base=-2 * BLOCK, channel_multiplier=BLOCK).then_inc(pool_step, 1)
            nc.gpsimd.iota(limit_i[:, 1:2], [[0, 1]], base=(P - 2) * BLOCK, channel_multiplier=BLOCK).then_inc(pool_step, 1)
            nc.gpsimd.memset(half[:, :], -0.5).then_inc(pool_step, 1)
            pool.wait_ge(pool_step, 5)
            nc.gpsimd.affine_select(out=ident[:, :], in_=ident[:, :], compare_op=ALU.not_equal, fill=1.0,
                                    base=0, pattern=[[-1, P]], channel_multiplier=1).then_inc(constants_ready, 1)
            nc.gpsimd.tensor_copy(limit[:, :], limit_i[:, :]).then_inc(constants_ready, 1)
            nc.gpsimd.tensor_copy(iota[:, :], iota_i[:, :]).then_inc(constants_ready, 1)
            nc.gpsimd.memset(aggT[:, :], 0.0).then_inc(agg_cleared, 1)
            pool.wait_ge(weights_landed, 16 * 4)

            pool.wait_ge(w1_hi_ready, 1)
            nc.gpsimd.tensor_tensor(w1_lo[:, :], w1[:, 0, :], w1_hi[:, :].bitcast(F32), ALU.subtract).then_inc(w1_ready, 1)

            def layernorm(b, par):
                w = width(b)
                pool.wait_ge(stats_ready, b + 1)
                nc.gpsimd.tensor_tensor(diff2[0:w, :], diff[0:w, par, :], diff[0:w, par, :], ALU.mult)
                nc.gpsimd.tensor_scalar(negmean[0:w, :], sums[0:w, par, :, 0], -0.5, 0.0, ALU.mult, ALU.add)
                nc.gpsimd.tensor_scalar(vareps[0:w, :], sums[0:w, par, :, 1], 4.0 / F, 4e-5, ALU.mult,
                                        ALU.add).then_inc(vareps_done, 1)
                pool.wait_ge(vareps_done, 3 * b + 1)
                nc.gpsimd.tensor_tensor(vareps[0:w, :], vareps[0:w, :], diff2[0:w, :], ALU.add).then_inc(vareps_done, 1)
                pool.wait_ge(vareps_done, 3 * b + 2)
                nc.gpsimd.tensor_tensor(rstd[0:w, par, :], vareps[0:w, :], half[0:w, :], ALU.pow).then_inc(vareps_done, 1)
                pool.wait_ge(vareps_done, 3 * b + 3)
                nc.gpsimd.tensor_tensor(shift[0:w, par, :], negmean[0:w, :], rstd[0:w, par, :],
                                        ALU.mult).then_inc(rstd_ready, 1)
                pool.wait_ge(xn_ready, b + 1)
                r = xs[0:w, bass.ds(b, 1), :].rearrange("p b (j f) -> p (b j) f", j=2)
                nc.gpsimd.tensor_tensor(r, r, b2_all[0:w, :].unsqueeze(1).to_broadcast([w, 2, F]),
                                        ALU.add).then_inc(residual_ready, 1)

            def step(s, par, q):
                landed(pool, s, par, q, 4)
                if not isinstance(s, int) or s > 0:
                    pool.wait_ge(chunk_summed, s * SC)
                take_apart(nc.gpsimd, pool, POOLED, par * SC + POOLED, s, pool_rem_ready, pool_low_ready)
                layernorm(s + 1, 1 - par)

            layernorm(0, 0)
            step(0, 0, 0)
            step(1, 1, 0)
            with pool.Fori(1, (STEPS - 2) // 2) as m:
                step(2 * m, 0, m)
                step(2 * m + 1, 1, m)
            step(STEPS - 2, 0, (STEPS - 2) // 2)
            layernorm(NB - 1, 0)

        @block.scalar
        def _(act):
            act.dma_start(xs[:, 0:3, :], x_v[:, 0:3, :]).then_inc(x_first_landed, 16)
            act.dma_start(b1_row[:, :], b1.rearrange("(t p) -> t p", p=P)).then_inc(weights_landed, 16)
            act.dma_start(b2_all[:, :], b2.partition_broadcast(P)).then_inc(weights_landed, 16)
            act.dma_start(w1[:, :, :], W1.rearrange("(t p) h -> p t h", p=P)).then_inc(weights_landed, 16)
            act.dma_start(w2[:, :, :], W2.rearrange("(t p) f -> p t f", p=P)).then_inc(weights_landed, 16)
            act.dma_start(xs[0:NLAST // 2, NB - 1, :], x_last_v).then_inc(x_last_landed, 16)

            def normalise(b, par):
                w = width(b)
                act.wait_ge(rstd_ready, b + 1)
                if not isinstance(b, int) or b >= 2:
                    act.wait_ge(h_turned, b - 1)
                for j in range(2):
                    ins = nc.scalar.activation(
                        xn[0:w, par, j, :], xs[0:w, bass.ds(b, 1), j * F:(j + 1) * F].rearrange("p b f -> p (b f)"),
                        ACT.Relu, bias=shift[0:w, par, j:j + 1], scale=rstd[0:w, par, j:j + 1])
                ins.then_inc(xn_ready, 1)

            def h_out(b):
                w = width(b)
                act.wait_ge(h_turned, b + 1)
                nc.scalar.activation(hT[:, bass.ds(b * BLOCK, 2 * w)], tr_ps[:, 0:2 * w], ACT.Copy,
                                     scale=2.0).then_inc(hT_ready, 1)

            def round_agg(n, par, b, added):
                w = width(b)
                act.wait_ge(agg_added, added)
                if not isinstance(n, int) or n >= 2:
                    act.wait_ge(hidden_summed, 2 * n - 2)
                nc.scalar.activation(agg_hi[:, par, 0:2 * w].rearrange("f (j p) -> f j p", j=2),
                                     aggT[:, bass.ds(b * BLOCK, 2 * w)].rearrange("f (p j) -> f j p", j=2),
                                     ACT.Copy).then_inc(agg_hi_ready, 1)

            def relu(n, par, b, first=False):
                w = width(b)
                for t in range(HT):
                    if t % 2 == 0:
                        act.wait_ge(hidden_summed, 2 * n + t // 2 + 1)
                    if t == 0 and not first:
                        act.wait_ge(out_summed, n - 1)
                    nc.scalar.activation(hidden[par][:, t, 0:2 * w],
                                         hid_ps[t // 2][:, (t % 2) * 2 * w:(t % 2 + 1) * 2 * w], ACT.Relu,
                                         bias=b1_col[:, t:t + 1]).then_inc(hidden_ready, 1)

            act.wait_ge(columns_turned, 1)
            nc.scalar.activation(b1_col[:, :], tr_ps[:, 0:HT], ACT.Copy).then_inc(hidden_ready, HT)
            act.wait_ge(hidden_ready, HT)
            nc.scalar.activation(w1_hi[:, :], w1[:, 0, :], ACT.Copy).then_inc(w1_hi_ready, 1)

            def step(s, par):
                h_out(s)
                if not isinstance(s, int) or s > 0:
                    round_agg(s - 1, 1 - par, s - 1, s * SC + 2)
                normalise(s + 1, 1 - par)
                if not isinstance(s, int) or s > 0:
                    relu(s - 1, 1 - par, s - 1, first=isinstance(s, int) and s < 3)

            normalise(0, 0)
            for s in range(3):
                step(s, s % 2)
            with act.Fori(1, (STEPS - 2) // 2) as m:
                step(2 * m + 1, 1)
                step(2 * m + 2, 0)
            step(STEPS - 1, 1)
            h_out(NB - 1)
            for b in (NB - 2, NB - 1):
                round_agg(b, b % 2, b, NCH)
            for b in (NB - 2, NB - 1):
                relu(b, b % 2, b)

            act.wait_ge(flag_ready, 1)
            again = act.value_load(flag[0:1, 0:1], min_val=0, max_val=1)
            with act.If(again > 0):
                act.wait_ge(wide_added, NCH * NWIDE + 1)

                def again_block(n, par, b):
                    round_agg(n, par, b, NCH)
                    relu(n, par, b)

                with act.Fori(0, (NB - 1) // 2) as i:
                    again_block(NB + 2 * i, 1, 2 * i)
                    again_block(NB + 2 * i + 1, 0, 2 * i + 1)
                again_block(2 * NB - 1, 1, NB - 1)

        @block.vector
        def _(dve):
            links = [0]

            def link(ins):
                links[0] += 1
                ins.then_inc(vec_step, 1)
                dve.wait_ge(vec_step, links[0])

            def build(c, s, k):
                hot = onehot[:, PLAIN.index(k), :, :] if plain(s, k) else onehot_h[:, HALVED.index(k), :, :]
                nc.vector.tensor_tensor(
                    hot, at(relT, c).rearrange("p c g -> p (c g)").unsqueeze(2).to_broadcast([P, G, W]),
                    iota[:, 0:W].unsqueeze(1).to_broadcast([P, G, W]), ALU.is_equal).then_inc(onehot_ready, 1)

            def statistics(b, par):
                w = width(b)
                for j in range(2):
                    ins = nc.vector.bn_stats(stats[0:w, j, :], xs[0:w, bass.ds(b, 1), j * F:(j + 1) * F]
                                             .rearrange("p b f -> p (b f)"))
                ins.then_inc(stats_done, 1)
                dve.wait_ge(stats_done, b + 1)
                nc.vector.tensor_tensor(sums[0:w, par, :, :], stats[0:w, :, 1:3], stats[0:w, :, 4:6], ALU.add)
                nc.vector.tensor_tensor(diff[0:w, par, :], stats[0:w, :, 1], stats[0:w, :, 4],
                                        ALU.subtract).then_inc(stats_ready, 1)

            def rest_of_agg(n, par, b):
                w = width(b)
                dve.wait_ge(agg_hi_ready, n + 1)
                split = lambda t: t.rearrange("f (j p) -> f j p", j=2)
                nc.vector.tensor_tensor(split(agg_lo[:, par, 0:2 * w]),
                                        aggT[:, bass.ds(b * BLOCK, 2 * w)].rearrange("f (p j) -> f j p", j=2),
                                        split(agg_hi[:, par, 0:2 * w].bitcast(F32)), ALU.subtract).then_inc(agg_lo_ready, 1)

            def parts(s, par, q, k):
                if plain(s, k) or k == POOLED:
                    return
                landed(dve, s, par, q, [k0 for k0, _ in PARTS if k0 <= k][-1])
                take_apart(nc.vector, dve, k, par * SC + k, s * (len(HALVED) - 1) + HALVED.index(k), rem_ready, low_ready)

            def add_chunk(c, base, slot, first=False):
                dve.wait_ge(chunk_summed, c + 1)
                if not first:
                    dve.wait_ge(agg_added, c)
                win = aggT[:, bass.ds(base, W)]
                nc.vector.tensor_tensor(win, chunk_ps[BANK[slot]][:, 0:W], win, ALU.add).then_inc(agg_added, 1)

            def finish(n, par, b, q, again=False):
                w = width(b)
                dve.wait_ge(out_summed, n + 1)
                if not again:
                    dve.wait_ge(residual_ready, n + 1)
                if not isinstance(q, int) or q > 0:
                    dve.wait_ge(stored[par], 16 * q)
                nc.vector.tensor_tensor(outrow[0:w, par, :], out_ps[0:w, 0:2 * F],
                                        xs[0:w, bass.ds(b, 1), :].rearrange("p b f -> p (b f)"),
                                        ALU.add).then_inc(out_added, 1)

            def step(s, par, q):
                last = is_last(s)
                _, bases = nc.values_load_multi_w_load_instructions(
                    base_tab[0:1, bass.ds(s, 1), :].rearrange("a s k -> a (s k)"), engines=[dve.engine], min_val=0,
                    max_val=N - 1, skip_runtime_bounds_check_because="clamped when written")
                for k in range(LASTC if last else SC):
                    c = s * SC + k
                    if k + LEAD < SC and (not last or k + LEAD < LASTC):
                        build(c + LEAD, s, k + LEAD)
                        parts(s, par, q, k + LEAD)
                    elif not last and not (is_last(s + 1) and k + LEAD - SC >= LASTC):
                        build(c + LEAD, s + 1, k + LEAD - SC)
                        parts(s + 1, 1 - par, q + par, k + LEAD - SC)
                    add_chunk(c, bases[k], par * SC + k, first=isinstance(c, int) and c == 0)
                    if k == 2 and (not isinstance(s, int) or s >= 1):
                        rest_of_agg(s - 1, 1 - par, s - 1)
                    if k == 3:
                        if last:
                            dve.wait_ge(x_last_landed, 16)
                        elif not isinstance(s, int) or s >= 2:
                            dve.wait_ge(x_landed[1 - par], 16 * q)
                        statistics(s + 1, 1 - par)
                    if k == 4 and (not isinstance(s, int) or s >= 2):
                        finish(s - 2, par, s - 2, q - 1)

            dve.wait_ge(dst_landed, 48)
            for d, col, rel in ((dstA, colA, relA), (dstB, colB, relB)):
                link(nc.vector.tensor_reduce(col[:, 0:1], d[:, :], AX_X, ALU.min))
                link(nc.vector.tensor_reduce(col[:, 1:2], d[:, :], AX_X, ALU.max))
                nc.vector.tensor_scalar(rel[:, :], d[:, :], col[:, 0:1], None, ALU.subtract).then_inc(rel_ready, 1)
            dve.wait_ge(constants_ready, 3)
            dve.wait_ge(rel_turned, 1)

            def turned(done):
                nc.vector.tensor_copy(relT[:, 0:P, 0:4].rearrange("p c g -> p g c"),
                                      chunk_ps[0][:, :].rearrange("p (g c) -> p g c", c=P))
                nc.vector.tensor_copy(relT[:, 0:P, 4], chunk_ps[1][:, 0:P])
                nc.vector.tensor_copy(relT[:, P:NCH, :].rearrange("p c g -> p g c"),
                                      chunk_ps[1][:, P:P + G * CB].rearrange("p (g c) -> p g c", c=CB)).then_inc(done, 1)

            turned(banks_free)
            for col, n, lim in ((colA, P, limit[:, 0:1]), (colB, CB, limit[0:CB, 1:2])):
                nc.vector.scalar_tensor_tensor(col[:, 2:3], col[:, 1:2], float(-(W - 1)), col[:, 0:1], ALU.add, ALU.subtract)
                link(nc.vector.scalar_tensor_tensor(col[:, 3:4], col[:, 0:1], float(-SC), lim, ALU.mult, ALU.add))
                nc.vector.tensor_tensor(col[:, 4:5], col[:, 2:3], col[:, 3:4], ALU.max).then_inc(rel_ready, 1)
            dve.wait_ge(columns_turned, 2)
            link(nc.vector.memset(base_row[:, :], 0))
            link(nc.vector.tensor_scalar(base_row[:, 0:NCH], hid_ps[0][0:1, 0:NCH], 0.0, float(N - 1), ALU.max, ALU.min))
            link(nc.vector.memset(base_tab[:, :, :], 0))
            nc.vector.tensor_copy(base_tab[:, :, 0:SC], base_row[:, :].rearrange("a (s k) -> a s k", k=SC))
            link(nc.vector.tensor_reduce(over[:, :], hid_ps[0][0:1, 256:256 + NCH], AX_X, ALU.max))
            nc.vector.tensor_scalar(flag[:, :], over[:, :], 0.0, None, ALU.is_gt).then_inc(flag_ready, 1)
            dve.wait_ge(flag_ready, 1)

            dve.wait_ge(x_first_landed, 16)
            statistics(0, 0)
            for c in range(LEAD):
                build(c, 0, c)
                parts(0, 0, 0, c)
            dve.wait_ge(agg_cleared, 1)
            for s in range(5):
                step(s, s % 2, s // 2)
            with dve.Fori(2, (STEPS - 4) // 2) as m:
                step(2 * m + 1, 1, m)
                step(2 * m + 2, 0, m + 1)
            for s in range(STEPS - 3, STEPS):
                step(s, s % 2, s // 2)
            for b in (NB - 2, NB - 1):
                rest_of_agg(b, b % 2, b)
            for b in range(NB - 3, NB):
                finish(b, b % 2, b, b // 2)

            again = dve.value_load(flag[0:1, 0:1], min_val=0, max_val=1)
            with dve.If(again > 0):
                for col, rel, d in ((colA, relA, dstA), (colB, relB, dstB)):
                    hot = edges[0:rel.shape[0], 1, 0:CHUNK]
                    nc.vector.tensor_scalar(hot, rel[:, :], float(W), None, ALU.is_ge).then_inc(wide_dst_ready, 1)
                    nc.vector.tensor_scalar(col[:, 5:6], col[:, 0:1], 1.0, None, ALU.add).then_inc(wide_dst_ready, 1)
                    dve.wait_ge(wide_dst_ready, 2 if rel is relA else 4)
                    nc.vector.scalar_tensor_tensor(rel[:, :], rel[:, :], col[:, 5:6], hot, ALU.add,
                                                   ALU.mult).then_inc(wide_rel_ready, 1)
                    dve.wait_ge(wide_rel_ready, 1 if rel is relA else 2)
                dve.wait_ge(wide_summed, 1)
                turned(wide_added)

                def wide(c):
                    with dve.Fori(0, NWIDE) as j:
                        n = c * NWIDE + j
                        dve.wait_ge(wide_added, n + 1)
                        nc.vector.tensor_scalar(wide_dst[:, :], at(relT, c).rearrange("p c g -> p (c g)"),
                                                wide_base[:, bass.ds(j, 1)], None, ALU.subtract).then_inc(wide_dst_ready, 1)
                        dve.wait_ge(wide_dst_ready, 4 + n + 1)
                        nc.vector.tensor_tensor(wide_hot[:, :, :], wide_dst[:, :].unsqueeze(2).to_broadcast([P, G, WIDE]),
                                                iota[:, :].unsqueeze(1).to_broadcast([P, G, WIDE]),
                                                ALU.is_equal).then_inc(wide_hot_ready, 1)
                        dve.wait_ge(wide_summed, n + 2)
                        win = aggT[:, bass.ds(j * WIDE, WIDE)]
                        nc.vector.tensor_tensor(win, chunk_ps[0][:, :], win, ALU.add).then_inc(wide_added, 1)

                wide_base = xn[:, 0, 0, 0:NWIDE]
                for j in range(NWIDE):
                    nc.vector.memset(wide_base[:, j:j + 1], float(j * WIDE + 1)).then_inc(wide_rel_ready, 1)
                dve.wait_ge(wide_rel_ready, 2 + NWIDE)
                with dve.Fori(0, NCH) as c:
                    wide(c)

                def again_block(n, par, b, q):
                    rest_of_agg(n, par, b)
                    finish(n, par, b, q, again=True)

                with dve.Fori(0, (NB - 1) // 2) as i:
                    again_block(NB + 2 * i, 1, 2 * i, i + NB // 2)
                    again_block(NB + 2 * i + 1, 0, 2 * i + 1, i + NB // 2 + 1)
                again_block(2 * NB - 1, 1, NB - 1, NB - 1)

        @block.tensor
        def _(pe):
            def turn_rel():
                for g in range(4):
                    nc.tensor.transpose(chunk_ps[0][:, g * P:(g + 1) * P], relA[:, g:CHUNK:G], ident[:, :])
                nc.tensor.transpose(chunk_ps[1][:, 0:P], relA[:, 4:CHUNK:G], ident[:, :])
                for g in range(G):
                    ins = nc.tensor.transpose(chunk_ps[1][:, P + g * CB:P + (g + 1) * CB], relB[:, g:CHUNK:G],
                                              ident[0:CB, 0:CB])
                return ins

            def sum_chunk(c, s, par, q, k):
                kp = KREST if isinstance(c, int) and c == NCH - 1 else P
                slot = par * SC + k
                landed(pe, s, par, q, k)
                pe.wait_ge(onehot_ready, c + 1)
                if not isinstance(c, int) or c >= SINCE[slot]:
                    pe.wait_ge(agg_added, c - SINCE[slot] + 1)
                sums_ps = chunk_ps[BANK[slot]][:, 0:W]
                if plain(s, k):
                    for g in range(G):
                        ins = nc.tensor.matmul(sums_ps, edges[0:kp, slot, g * F:(g + 1) * F],
                                               onehot[0:kp, PLAIN.index(k), g, :], start=(g == 0), stop=(g == G - 1))
                else:
                    i = HALVED.index(k)
                    if k == POOLED:
                        pe.wait_ge(pool_low_ready, s + 1)
                    else:
                        pe.wait_ge(low_ready, s * (len(HALVED) - 1) + i + 1)
                    high, middle = upper(edges[:, slot, :]), upper(rem[:, i, :])
                    for g in range(G):
                        hot, cols = onehot_h[:, i, g, :], slice(g * F, (g + 1) * F)
                        nc.tensor.matmul(sums_ps, high[:, cols], hot, start=(g == 0), stop=False)
                        nc.tensor.matmul(sums_ps, middle[:, cols], hot, start=False, stop=False)
                        ins = nc.tensor.matmul(sums_ps, low[:, i, cols], hot, start=False, stop=(g == G - 1))
                ins.then_inc(chunk_summed, 1)

            def turn_x(b, par, first=False):
                w = width(b)
                pe.wait_ge(xn_ready, b + 1)
                if not first:
                    pe.wait_ge(hT_ready, b)
                for j in range(2):
                    ins = nc.tensor.transpose(tr_ps[:, j * w:(j + 1) * w], xn[0:w, par, j, :], ident[0:w, 0:w])
                ins.then_inc(h_turned, 1)

            def layer1(n, par, b):
                w = width(b)
                pe.wait_ge(agg_lo_ready, n + 1)
                for t in range(HT):
                    if t % 2 == 0:
                        pe.wait_ge(hidden_ready, n * HT + t + 2)
                    o = hid_ps[t // 2][:, (t % 2) * 2 * w:(t % 2 + 1) * 2 * w]
                    cols = slice(t * P, (t + 1) * P)
                    nc.tensor.matmul(o, w1[:, 1, cols], hT[:, bass.ds(b * BLOCK, 2 * w)], start=True, stop=False)
                    nc.tensor.matmul(o, w1_hi[:, cols], agg_hi[:, par, 0:2 * w], start=False, stop=False)
                    nc.tensor.matmul(o, w1_hi[:, cols], agg_lo[:, par, 0:2 * w], start=False, stop=False)
                    ins = nc.tensor.matmul(o, w1_lo[:, cols], agg_hi[:, par, 0:2 * w], start=False, stop=True)
                    if t % 2 == 1:
                        ins.then_inc(hidden_summed, 1)

            def layer2(n, par, b):
                w = width(b)
                if not isinstance(n, int) or n > 0:
                    pe.wait_ge(out_added, n)
                for j in range(2):
                    for t in range(HT):
                        if j == 0:
                            pe.wait_ge(hidden_ready, (n + 1) * HT + t + 1)
                        ins = nc.tensor.matmul(out_ps[0:w, j * F:(j + 1) * F], hidden[par][:, t, j * w:(j + 1) * w],
                                               w2[:, t, :], start=(t == 0), stop=(t == HT - 1))
                ins.then_inc(out_summed, 1)

            def step(s, par, q):
                for k in range(LASTC if is_last(s) else SC):
                    sum_chunk(s * SC + k, s, par, q, k)
                    if k == 0:
                        turn_x(s, par, first=isinstance(s, int) and s == 0)
                    if k == 1 and (not isinstance(s, int) or s >= 2):
                        layer2(s - 2, par, s - 2)
                    if k == (LASTC if is_last(s) else SC) - 1 and (not isinstance(s, int) or s >= 1):
                        pe.wait_ge(hT_ready, s)
                        layer1(s - 1, 1 - par, s - 1)

            pe.wait_ge(constants_ready, 1)
            pe.wait_ge(weights_landed, 64)
            nc.tensor.transpose(tr_ps[:, 0:HT], b1_row[:, :], ident[0:HT, 0:HT]).then_inc(columns_turned, 1)
            pe.wait_ge(rel_ready, 2)
            turn_rel().then_inc(rel_turned, 1)
            pe.wait_ge(rel_ready, 4)
            for i, col in ((0, 0), (256, 4)):
                nc.tensor.transpose(hid_ps[0][0:1, i:i + P], colA[:, col:col + 1], ident[:, :])
                ins = nc.tensor.transpose(hid_ps[0][0:1, i + P:i + NCH], colB[:, col:col + 1], ident[0:CB, 0:CB])
            ins.then_inc(columns_turned, 1)
            pe.wait_ge(banks_free, 1)
            pe.wait_ge(hidden_ready, HT)
            pe.wait_ge(flag_ready, 1)

            pe.wait_ge(w1_ready, 1)
            for s in range(3):
                step(s, s % 2, s // 2)
            with pe.Fori(1, (STEPS - 2) // 2) as m:
                step(2 * m + 1, 1, m)
                step(2 * m + 2, 0, m + 1)
            step(STEPS - 1, 1, (STEPS - 1) // 2)
            turn_x(NB - 1, 0)
            layer2(NB - 3, 0, NB - 3)
            pe.wait_ge(hT_ready, NB)
            for b in (NB - 2, NB - 1):
                layer1(b, b % 2, b)
            for b in (NB - 2, NB - 1):
                layer2(b, b % 2, b)

            again = pe.value_load(flag[0:1, 0:1], min_val=0, max_val=1)
            with pe.If(again > 0):
                pe.wait_ge(wide_rel_ready, 2)
                turn_rel().then_inc(wide_summed, 1)

                def wide(c, kp):
                    with pe.Fori(0, NWIDE) as j:
                        n = c * NWIDE + j
                        pe.wait_ge(wide_landed, 16 * (c + 1))
                        pe.wait_ge(wide_hot_ready, n + 1)
                        for g in range(G):
                            ins = nc.tensor.matmul(chunk_ps[0][:, :], edges[0:kp, 0, g * F:(g + 1) * F],
                                                   wide_hot[0:kp, g, :], start=(g == 0), stop=(g == G - 1))
                        ins.then_inc(wide_summed, 1)

                with pe.Fori(0, FULL) as c:
                    wide(c, P)
                wide(FULL, KREST)

                def again_block(n, par, b):
                    layer1(n, par, b)
                    layer2(n, par, b)

                with pe.Fori(0, (NB - 1) // 2) as i:
                    again_block(NB + 2 * i, 1, 2 * i)
                    again_block(NB + 2 * i + 1, 0, 2 * i + 1)
                again_block(2 * NB - 1, 1, NB - 1)


_INS = ["x", "dst", "edge_attr_128", "L0_gnn_W1", "L0_gnn_b1", "L0_gnn_W2", "L0_gnn_b2"]


def kernel(**inputs):
    import numpy as _np
    import concourse.bacc as _bacc
    from concourse import mybir as _mybir
    from concourse.bass_utils import run_bass_kernel_spmd as _run

    nc = _bacc.Bacc("TRN2", target_bir_lowering=False, num_devices=1)
    arrays, args = {}, []
    for name in _INS:
        a = _np.ascontiguousarray(inputs[name])
        arrays[f"in_{name}"] = a
        args.append(nc.dram_tensor(f"in_{name}", a.shape, _mybir.dt.from_np(a.dtype), kind="ExternalInput").ap())
    out = nc.dram_tensor("out_rows", inputs["x"].shape, F32, kind="ExternalOutput").ap()
    graph_layer(nc, *args, out)
    r = _run(nc, [arrays], core_ids=[0])
    return r.results[0]["out_rows"]
```

```python
from contextlib import ExitStack

import concourse.bass as bass
from concourse import mybir

P = 128
F32 = mybir.dt.float32
F32R = mybir.dt.float32r
BF16 = mybir.dt.bfloat16
I32 = mybir.dt.int32
ALU = mybir.AluOpType
ACT = mybir.ActivationFunctionType
AX_X = mybir.AxisListType.X

G = 5
CHUNK = P * G
W = 48
SC = 7
BLOCK = 2 * P
LEAD = 6
WIDE = 512
PARTS = [(0, 2), (2, 2), (4, 3)]
BANK = [0, 1, 2, 3, 0, 1, 2, 3, 0, 1, 2, 0, 1, 2]
PLAIN = [0, 3, 2]
HALVED = [1, 2, 4, 5, 6]
POOLED = 6
APART = [[1, 2, 4, 5], [1, 4, 5]]
SINCE = [next(d for d in range(1, 15) if BANK[(i - d) % 14] == BANK[i]) for i in range(14)]


def graph_layer(nc, x, dst, edge_attr, W1, b1, W2, b2, out):
    N, F = x.shape
    E = edge_attr.shape[0]
    H = W1.shape[1]
    HT = H // P
    FULL = E // CHUNK
    REST = E - FULL * CHUNK
    KREST = REST // G
    NCH = FULL + 1
    NB = -(-N // BLOCK)
    NLAST = N - (NB - 1) * BLOCK
    STEPS = NB - 1
    CA, CB = P, NCH - P
    NWIDE = -(-N // WIDE)
    assert F == P and H == HT * P and HT == 4
    assert REST == KREST * G and 0 < KREST <= P and CHUNK % REST == 0
    assert STEPS % 2 == 0 and (STEPS - 1) * SC < NCH <= STEPS * SC and NLAST % 2 == 0
    HALF_AGG = NWIDE // 2 * WIDE
    LASTC = NCH - (STEPS - 1) * SC
    assert LASTC == 6

    def width(b):
        return NLAST // 2 if isinstance(b, int) and b == NB - 1 else P

    with ExitStack() as ctx:
        def sb(name, shape, dt=F32):
            return ctx.enter_context(nc.sbuf_tensor(name, shape, dt))

        def sem(name):
            return ctx.enter_context(nc.semaphore(name))

        edges = sb("edges", [P, 2 * SC, G * F])
        aggT = sb("aggT", [P, NWIDE * WIDE])
        hT_hi = sb("hT_hi", [P, NB * BLOCK], F32R)
        hT_lo = sb("hT_lo", [P, NB * BLOCK], F32R)
        xs = sb("xs", [P, NB, 2 * F])
        relA = sb("relA", [P, CHUNK])
        relB = sb("relB", [CB, CHUNK])
        relT = sb("relT", [P, STEPS * SC, G])
        relT_h = sb("relT_h", [P, STEPS * SC, G], BF16)
        colA = sb("colA", [P, 6])
        colB = sb("colB", [CB, 6])
        limit = sb("limit", [P, 2])
        limit_i = sb("limit_i", [P, 2], I32)
        base_tab = sb("base_tab", [1, STEPS, 8], I32)
        over = sb("over", [1, 1])
        flag = sb("flag", [1, 1], I32)
        onehot = sb("onehot", [P, len(PLAIN), G, W])
        onehot_h = sb("onehot_h", [P, len(HALVED), W, G], BF16)
        rem = sb("rem", [P, len(HALVED), G * F])
        low = sb("low", [P, len(HALVED), G * F], BF16)
        iota = sb("iota", [P, WIDE])
        iota_h = sb("iota_h", [P, W, G], BF16)
        ident = sb("ident", [P, P])
        w1 = sb("w1", [P, 2, H])
        w1_hi = sb("w1_hi", [P, 2, H], F32R)
        w1_lo = sb("w1_lo", [P, 2, H], F32R)
        agg_hi = sb("agg_hi", [P, 2, BLOCK], F32R)
        agg_lo = sb("agg_lo", [P, 2, BLOCK], F32R)
        w2 = sb("w2", [P, HT, F])
        b1_row = sb("b1_row", [HT, P])
        b1_col = sb("b1_col", [P, HT])
        b2_all = sb("b2_all", [P, F])
        negmean = sb("negmean", [P, 2, 2])
        squares = sb("squares", [P, 2, 2])
        var = sb("var", [P, 2])
        vareps = sb("vareps", [P, 2])
        rstd = sb("rstd", [P, 2, 2])
        shift = sb("shift", [P, 2, 2])
        coef = sb("coef", [P, 3, 2])
        xn = sb("xn", [P, 2, 2, F])
        hidden = [sb(f"hidden{i}", [P, HT, BLOCK]) for i in range(2)]
        outrow = sb("outrow", [P, 2, 2 * F])
        early = [h[:, :, :].rearrange("p t n -> p (t n)").bitcast(I32) for h in hidden]
        dstA = early[0][:, 0:CHUNK]
        dstB = early[1][0:CB, 0:CHUNK]
        iota_wi = early[0][:, CHUNK:CHUNK + W * G].rearrange("p (w g) -> p w g", g=G)
        iota_i = xn[:, :, :, :].rearrange("p a b n -> p (a b n)").bitcast(I32)
        wide_hot = edges[:, 2:6, :].rearrange("p a b -> p (a b)").rearrange("p (g w) -> p g w", g=G)
        wide_dst = sb("wide_dst", [P, G])

        bank = [ctx.enter_context(nc.psum_tensor(f"bank{i}", [P, 512], F32)) for i in range(8)]
        chunk_ps = bank[0:4]
        hid_ps = bank[4:6]
        tr_ps = bank[6]
        out_ps = bank[7]
        bases_ps = bank[3]

        dst_landed = [sem(f"dst_landed{i}") for i in range(2)]
        x_first_landed = sem("x_first_landed")
        x_landed = [sem(f"x_landed{i}") for i in range(2)]
        x_last_landed = sem("x_last_landed")
        weights_landed = sem("weights_landed")
        edges_landed = [sem(f"edges_landed{i}") for i in range(2 * len(PARTS))]
        constants_ready = sem("constants_ready")
        iota_i_ready = sem("iota_i_ready")
        iota_ready = sem("iota_ready")
        agg_cleared = sem("agg_cleared")
        rel_ready = sem("rel_ready")
        overrun_ready = sem("overrun_ready")
        rel_turned = sem("rel_turned")
        columns_turned = sem("columns_turned")
        rel_copied = sem("rel_copied")
        bases_ready = sem("bases_ready")
        flag_ready = sem("flag_ready")
        onehot_ready = sem("onehot_ready")
        chunk_summed = sem("chunk_summed")
        agg_added = sem("agg_added")
        means_ready = sem("means_ready")
        squares_ready = sem("squares_ready")
        var_step = sem("var_step")
        rstd_ready = sem("rstd_ready")
        xn_ready = sem("xn_ready")
        residual_ready = sem("residual_ready")
        w1_hi_ready = sem("w1_hi_ready")
        w1_ready = sem("w1_ready")
        rem_ready = sem("rem_ready")
        low_ready = sem("low_ready")
        pool_rem_ready = sem("pool_rem_ready")
        pool_low_ready = sem("pool_low_ready")
        agg_hi_ready = sem("agg_hi_ready")
        agg_lo_ready = sem("agg_lo_ready")
        h_turned = sem("h_turned")
        hT_hi_ready = sem("hT_hi_ready")
        hT_lo_ready = sem("hT_lo_ready")
        hidden_summed = sem("hidden_summed")
        hidden_ready = sem("hidden_ready")
        out_summed = sem("out_summed")
        out_copied = sem("out_copied")
        out_added = sem("out_added")
        stored = [sem(f"stored{i}") for i in range(2)]
        vec_step = sem("vec_step")
        pool_step = sem("pool_step")
        wide_dst_ready = sem("wide_dst_ready")
        wide_rel_ready = sem("wide_rel_ready")
        wide_landed = sem("wide_landed")
        wide_hot_ready = sem("wide_hot_ready")
        wide_summed = sem("wide_summed")
        wide_added = sem("wide_added")

        chunks_v = edge_attr[0:FULL * CHUNK, :].rearrange("(c p g) f -> p c (g f)", p=P, g=G)
        rest_v = edge_attr[FULL * CHUNK:E, :].rearrange("(p g) f -> p (g f)", g=G)
        x_v = x[0:(NB - 1) * BLOCK, :].rearrange("(b p j) f -> p b (j f)", p=P, j=2)
        x_last_v = x[(NB - 1) * BLOCK:N, :].rearrange("(p j) f -> p (j f)", j=2)
        out_v = out[0:(NB - 1) * BLOCK, :].rearrange("(b p j) f -> p b (j f)", p=P, j=2)
        out_last_v = out[(NB - 1) * BLOCK:N, :].rearrange("(p j) f -> p (j f)", j=2)

        def at(t, i, n=1):
            return t[:, bass.ds(i, n)]

        def landed(eng, s, par, q, k):
            for i, (k0, n) in enumerate(PARTS):
                if k == k0:
                    eng.wait_ge(edges_landed[par * len(PARTS) + i], 16 * (q + 1))
            if isinstance(s, int) and s == STEPS - 1 and k == LASTC - 1:
                eng.wait_ge(edges_landed[par * len(PARTS) + 2], 16 * (q + 2))

        def is_last(s):
            return isinstance(s, int) and s == STEPS - 1

        def plain(par, k):
            return k != POOLED and k not in APART[par]

        def apart_before(par, q, k):
            return q * (len(APART[0]) + len(APART[1])) + par * len(APART[0]) + APART[par].index(k)

        def upper(t):
            n = t.shape[-1]
            return t.bitcast(BF16)[:, 1:2 * n:2]

        def take_apart(ops, eng, k, slot, n, rem_sem, low_sem, between=lambda: None):
            i = HALVED.index(k)
            e = edges[:, slot, :]
            ops.tensor_tensor(rem[:, i, :], e, upper(e), ALU.subtract).then_inc(rem_sem, 1)
            between()
            eng.wait_ge(rem_sem, n + 1)
            ops.tensor_tensor(low[:, i, :], rem[:, i, :], upper(rem[:, i, :]), ALU.subtract).then_inc(low_sem, 1)

        block = ctx.enter_context(nc.Block())

        @block.sync
        def _(sp):
            sp.dma_start(dstA[:, :], dst[0:P * CHUNK].rearrange("(c e) -> c e", e=CHUNK)).then_inc(dst_landed[0], 16)
            sp.dma_start(dstB[0:CB - 1, :],
                         dst[P * CHUNK:FULL * CHUNK].rearrange("(c e) -> c e", e=CHUNK)).then_inc(dst_landed[1], 16)
            rest = dst[FULL * CHUNK:E].rearrange("(a c e) -> a c e", a=1, c=1)
            sp.dma_start(dstB[CB - 1:CB, :].rearrange("a (c e) -> a c e", e=REST),
                         rest.to_broadcast([1, CHUNK // REST, REST])).then_inc(dst_landed[1], 16)

            def load(s, par, i, refill=True):
                k0, n = PARTS[i]
                if refill:
                    sp.wait_ge(chunk_summed, (s - 2) * SC + k0 + n)
                sp.dma_start(edges[:, par * SC + k0:par * SC + k0 + n, :],
                             chunks_v[:, bass.ds(s * SC + k0, n), :]
                             ).then_inc(edges_landed[par * len(PARTS) + i], 16)

            def load_x(b, par, q):
                if not isinstance(q, int) or q > 0:
                    sp.wait_ge(x_landed[par], 16 * q)
                sp.dma_start(xs[:, bass.ds(b, 1), :], x_v[:, bass.ds(b, 1), :]).then_inc(x_landed[par], 16)

            def store(n, par, b=None):
                b = n if b is None else b
                sp.wait_ge(out_added, n + 1)
                w = width(b)
                if w == P:
                    sp.dma_start(out_v[:, bass.ds(b, 1), :], outrow[:, par:par + 1, :]).then_inc(stored[par], 16)
                else:
                    sp.dma_start(out_last_v, outrow[0:w, par, :]).then_inc(stored[par], 16)

            for s in range(2):
                for i in range(len(PARTS)):
                    load(s, s, i, refill=False)
            for s in (2, 3):
                for i in range(len(PARTS)):
                    load(s, s % 2, i)
                load_x(s + 1, (s + 1) % 2, 0)
            with sp.Fori(0, 9) as m:
                for par in range(2):
                    s = 2 * m + 4 + par
                    load(s, par, 0)
                    load(s, par, 1)
                    load_x(s + 1, 1 - par, m + 1)
                    store(s - 4, par)
                    load(s, par, 2)
            s = STEPS - 2
            for i in range(len(PARTS)):
                load(s, 0, i)
            load_x(s + 1, 1, 10)
            store(s - 4, 0)
            s = STEPS - 1
            load(s, 1, 0)
            load(s, 1, 1)
            sp.wait_ge(chunk_summed, (s - 2) * SC + 6)
            sp.dma_start(edges[:, SC + 4, :], chunks_v[:, FULL - 1, :]).then_inc(edges_landed[5], 16)
            sp.wait_ge(edges_landed[5], 16 * 12)
            sp.dma_start(edges[0:KREST, SC + 5, :], rest_v).then_inc(edges_landed[5], 16)
            for b in range(s - 4, NB):
                store(b, b % 2)
            sp.wait_ge(stored[0], 16 * 13)
            sp.wait_ge(stored[1], 16 * 12)

            sp.wait_ge(flag_ready, 1)
            again = sp.value_load(flag[0:1, 0:1], min_val=0, max_val=1)
            with sp.If(again > 0):
                with sp.Fori(0, FULL) as c:
                    sp.wait_ge(wide_summed, c * NWIDE + 1)
                    sp.dma_start(edges[:, 0:1, :], chunks_v[:, bass.ds(c, 1), :]).then_inc(wide_landed, 16)
                sp.wait_ge(wide_summed, FULL * NWIDE + 1)
                sp.dma_start(edges[0:KREST, 0, :], rest_v).then_inc(wide_landed, 16)
                with sp.Fori(0, (NB - 1) // 2) as i:
                    store(NB + 2 * i, 1, 2 * i)
                    store(NB + 2 * i + 1, 0, 2 * i + 1)
                store(2 * NB - 1, 1, NB - 1)
                sp.wait_ge(stored[0], 16 * NB)
                sp.wait_ge(stored[1], 16 * NB)

        @block.gpsimd
        def _(pool):
            nc.gpsimd.memset(ident[:, :], 0.0).then_inc(pool_step, 1)
            nc.gpsimd.iota(iota_i[:, :], [[1, WIDE]], base=0, channel_multiplier=0).then_inc(iota_i_ready, 1)
            nc.gpsimd.iota(iota_wi[:, :, :], [[1, W], [0, G]], base=0, channel_multiplier=0).then_inc(iota_i_ready, 1)
            nc.gpsimd.iota(limit_i[:, 0:1], [[0, 1]], base=-2 * BLOCK, channel_multiplier=BLOCK).then_inc(pool_step, 1)
            nc.gpsimd.iota(limit_i[:, 1:2], [[0, 1]], base=(P - 2) * BLOCK, channel_multiplier=BLOCK).then_inc(pool_step, 1)
            for i, value in enumerate((1.0 / F, 1e-5, -0.5)):
                nc.gpsimd.memset(coef[:, i, :], value).then_inc(pool_step, 1)
            pool.wait_ge(pool_step, 6)
            nc.gpsimd.affine_select(out=ident[:, :], in_=ident[:, :], compare_op=ALU.not_equal, fill=1.0,
                                    base=0, pattern=[[-1, P]], channel_multiplier=1).then_inc(constants_ready, 1)
            nc.gpsimd.tensor_copy(limit[:, :], limit_i[:, :]).then_inc(constants_ready, 1)

            def layernorm(b, par):
                w = width(b)
                pool.wait_ge(squares_ready, b + 1)
                nc.gpsimd.tensor_tensor(var[0:w, :], squares[0:w, par, :], coef[0:w, 0, :], ALU.mult).then_inc(var_step, 1)
                pool.wait_ge(var_step, 3 * b + 1)
                nc.gpsimd.tensor_tensor(vareps[0:w, :], var[0:w, :], coef[0:w, 1, :], ALU.add).then_inc(var_step, 1)
                pool.wait_ge(var_step, 3 * b + 2)
                nc.gpsimd.tensor_tensor(rstd[0:w, par, :], vareps[0:w, :], coef[0:w, 2, :], ALU.pow).then_inc(var_step, 1)
                pool.wait_ge(var_step, 3 * b + 3)
                nc.gpsimd.tensor_tensor(shift[0:w, par, :], negmean[0:w, par, :], rstd[0:w, par, :],
                                        ALU.mult).then_inc(rstd_ready, 1)

            def add_b2(b):
                w = width(b)
                pool.wait_ge(xn_ready, b + 1)
                r = xs[0:w, bass.ds(b, 1), :].rearrange("p b (j f) -> p (b j) f", j=2)
                nc.gpsimd.tensor_tensor(r, r, b2_all[0:w, :].unsqueeze(1).to_broadcast([w, 2, F]),
                                        ALU.add).then_inc(residual_ready, 1)

            def finish(n, par, b, again=False):
                w = width(b)
                pool.wait_ge(out_copied, n + 1)
                pool.wait_ge(residual_ready, NB if again else b + 1)
                row = outrow[0:w, par, :]
                nc.gpsimd.tensor_tensor(row, row, xs[0:w, bass.ds(b, 1), :].rearrange("p b f -> p (b f)"),
                                        ALU.add).then_inc(out_added, 1)

            def step(s, par, q):
                landed(pool, s, par, q, 4)
                if not isinstance(s, int) or s > 0:
                    pool.wait_ge(chunk_summed, s * SC)
                take_apart(nc.gpsimd, pool, POOLED, par * SC + POOLED, s, pool_rem_ready, pool_low_ready)
                layernorm(s + 1, 1 - par)
                add_b2(s + 1)
                if not isinstance(s, int) or s >= 2:
                    finish(s - 2, par, s - 2)

            layernorm(0, 0)
            nc.gpsimd.memset(aggT[:, HALF_AGG:], 0.0).then_inc(agg_cleared, 1)
            pool.wait_ge(weights_landed, 16 * 4)
            add_b2(0)
            step(0, 0, 0)
            pool.wait_ge(w1_hi_ready, 1)
            nc.gpsimd.tensor_tensor(w1_lo[:, :, :], w1[:, :, :], w1_hi[:, :, :].bitcast(F32), ALU.subtract).then_inc(w1_ready, 1)
            step(1, 1, 0)
            step(2, 0, 1)
            step(3, 1, 1)
            with pool.Fori(2, (STEPS - 2) // 2) as m:
                step(2 * m, 0, m)
                step(2 * m + 1, 1, m)
            step(STEPS - 2, 0, (STEPS - 2) // 2)
            layernorm(NB - 1, 0)
            add_b2(NB - 1)
            for b in range(NB - 4, NB):
                finish(b, b % 2, b)

            pool.wait_ge(flag_ready, 1)
            again = pool.value_load(flag[0:1, 0:1], min_val=0, max_val=1)
            with pool.If(again > 0):
                with pool.Fori(0, (NB - 1) // 2) as i:
                    finish(NB + 2 * i, 1, 2 * i, again=True)
                    finish(NB + 2 * i + 1, 0, 2 * i + 1, again=True)
                finish(2 * NB - 1, 1, NB - 1, again=True)

        @block.scalar
        def _(act):
            act.dma_start(xs[:, 0:3, :], x_v[:, 0:3, :]).then_inc(x_first_landed, 16)
            act.dma_start(b1_row[:, :], b1.rearrange("(t p) -> t p", p=P)).then_inc(weights_landed, 16)
            act.dma_start(b2_all[:, :], b2.partition_broadcast(P)).then_inc(weights_landed, 16)
            act.wait_ge(iota_i_ready, 2)
            nc.scalar.activation(iota_h[:, :, :], iota_wi[:, :, :], ACT.Copy).then_inc(iota_ready, 1)
            nc.scalar.activation(iota[:, :], iota_i[:, :], ACT.Copy).then_inc(iota_ready, 1)

            act.dma_start(w1[:, :, :], W1.rearrange("(t p) h -> p t h", p=P)).then_inc(weights_landed, 16)
            act.dma_start(w2[:, :, :], W2.rearrange("(t p) f -> p t f", p=P)).then_inc(weights_landed, 16)
            act.dma_start(xs[0:NLAST // 2, NB - 1, :], x_last_v).then_inc(x_last_landed, 16)

            def row_of_x(b, j):
                return xs[0:width(b), bass.ds(b, 1), j * F:(j + 1) * F].rearrange("p b f -> p (b f)")

            def means(b, par):
                w = width(b)
                for j in range(2):
                    ins = nc.scalar.activation(xn[0:w, par, j, :], row_of_x(b, j), ACT.Copy, scale=-1.0 / F,
                                               accum_out=negmean[0:w, par, j:j + 1])
                ins.then_inc(means_ready, 1)

            def sum_squares(b, par):
                w = width(b)
                for j in range(2):
                    ins = nc.scalar.activation(xn[0:w, par, j, :], row_of_x(b, j), ACT.Square,
                                               bias=negmean[0:w, par, j:j + 1], accum_out=squares[0:w, par, j:j + 1])
                ins.then_inc(squares_ready, 1)

            def normalise(b, par):
                w = width(b)
                for j in range(2):
                    ins = nc.scalar.activation(
                        xn[0:w, par, j, :], xs[0:w, bass.ds(b, 1), j * F:(j + 1) * F].rearrange("p b f -> p (b f)"),
                        ACT.Relu, bias=shift[0:w, par, j:j + 1], scale=rstd[0:w, par, j:j + 1])
                ins.then_inc(xn_ready, 1)

            def h_out(b):
                w = width(b)
                act.wait_ge(h_turned, b + 1)
                nc.scalar.activation(hT_hi[:, bass.ds(b * BLOCK, 2 * w)], tr_ps[:, 0:2 * w],
                                     ACT.Copy).then_inc(hT_hi_ready, 1)

            def copy_out(n, par, b, q):
                w = width(b)
                act.wait_ge(out_summed, n + 1)
                if not isinstance(q, int) or q > 0:
                    act.wait_ge(stored[par], 16 * q)
                nc.scalar.activation(outrow[0:w, par, :], out_ps[0:w, 0:2 * F], ACT.Copy).then_inc(out_copied, 1)

            def round_agg(n, par, b, added):
                w = width(b)
                act.wait_ge(agg_added, added)
                if not isinstance(n, int) or n >= 2:
                    act.wait_ge(hidden_summed, 2 * n - 2)
                nc.scalar.activation(agg_hi[:, par, 0:2 * w].rearrange("f (j p) -> f j p", j=2),
                                     aggT[:, bass.ds(b * BLOCK, 2 * w)].rearrange("f (p j) -> f j p", j=2),
                                     ACT.Copy).then_inc(agg_hi_ready, 1)

            def relu(n, par, b, first=False):
                w = width(b)
                for t in range(HT):
                    if t % 2 == 0:
                        act.wait_ge(hidden_summed, 2 * n + t // 2 + 1)
                    if t == 0 and not first:
                        act.wait_ge(out_summed, n - 1)
                    nc.scalar.activation(hidden[par][:, t, 0:2 * w],
                                         hid_ps[t // 2][:, (t % 2) * 2 * w:(t % 2 + 1) * 2 * w], ACT.Relu,
                                         bias=b1_col[:, t:t + 1]).then_inc(hidden_ready, 1)

            def step(s, par, q):
                if is_last(s):
                    act.wait_ge(x_last_landed, 16)
                elif not isinstance(s, int) or s >= 2:
                    act.wait_ge(x_landed[1 - par], 16 * q)
                h_out(s)
                means(s + 1, 1 - par)
                act.wait_ge(means_ready, s + 2)
                if not isinstance(s, int) or s > 0:
                    round_agg(s - 1, 1 - par, s - 1, s * SC + 2)
                sum_squares(s + 1, 1 - par)
                act.wait_ge(rstd_ready, s + 2)
                if not isinstance(s, int) or s >= 2:
                    copy_out(s - 2, par, s - 2, q - 1)
                normalise(s + 1, 1 - par)
                if is_last(s):
                    round_agg(s, par, s, NCH)
                if not isinstance(s, int) or s > 0:
                    relu(s - 1, 1 - par, s - 1, first=isinstance(s, int) and s < 3)

            act.wait_ge(iota_ready, 2)
            act.wait_ge(x_first_landed, 16)
            means(0, 0)
            act.wait_ge(means_ready, 1)
            sum_squares(0, 0)
            act.wait_ge(rstd_ready, 1)
            normalise(0, 0)
            act.wait_ge(weights_landed, 64)
            nc.scalar.activation(w1_hi[:, :, :], w1[:, :, :], ACT.Copy).then_inc(w1_hi_ready, 1)
            step(0, 0, 0)
            act.wait_ge(columns_turned, 2)
            nc.scalar.activation(b1_col[:, :], hid_ps[0][:, 0:HT], ACT.Copy).then_inc(hidden_ready, HT)
            act.wait_ge(hidden_ready, HT)
            for s in (1, 2):
                step(s, s % 2, s // 2)
            with act.Fori(1, (STEPS - 2) // 2) as m:
                step(2 * m + 1, 1, m)
                step(2 * m + 2, 0, m + 1)
            step(STEPS - 1, 1, (STEPS - 1) // 2)
            h_out(NB - 1)
            copy_out(NB - 3, 0, NB - 3, (NB - 3) // 2)
            round_agg(NB - 1, 0, NB - 1, NCH)
            for b in (NB - 2, NB - 1):
                relu(b, b % 2, b)
            for b in (NB - 2, NB - 1):
                copy_out(b, b % 2, b, b // 2)

            act.wait_ge(flag_ready, 1)
            again = act.value_load(flag[0:1, 0:1], min_val=0, max_val=1)
            with act.If(again > 0):
                act.wait_ge(wide_added, NCH * NWIDE + 1)

                def again_block(n, par, b, q):
                    round_agg(n, par, b, NCH)
                    relu(n, par, b)
                    copy_out(n, par, b, q)

                with act.Fori(0, (NB - 1) // 2) as i:
                    again_block(NB + 2 * i, 1, 2 * i, i + NB // 2)
                    again_block(NB + 2 * i + 1, 0, 2 * i + 1, i + NB // 2 + 1)
                again_block(2 * NB - 1, 1, NB - 1, NB - 1)

        @block.vector
        def _(dve):
            links = [0]

            def link(ins):
                links[0] += 1
                ins.then_inc(vec_step, 1)
                dve.wait_ge(vec_step, links[0])

            def build(c, par, k):
                if not plain(par, k):
                    nc.vector.tensor_tensor(
                        onehot_h[:, HALVED.index(k), :, :], at(relT_h, c).to_broadcast([P, W, G]), iota_h[:, :, :],
                        ALU.is_equal).then_inc(onehot_ready, 1)
                    return
                hot = onehot[:, PLAIN.index(k), :, :]
                nc.vector.tensor_tensor(
                    hot, at(relT, c).rearrange("p c g -> p (c g)").unsqueeze(2).to_broadcast([P, G, W]),
                    iota[:, 0:W].unsqueeze(1).to_broadcast([P, G, W]), ALU.is_equal).then_inc(onehot_ready, 1)

            def rest_of_h(b):
                w = width(b)
                dve.wait_ge(hT_hi_ready, b + 1)
                cols = bass.ds(b * BLOCK, 2 * w)
                nc.vector.tensor_tensor(hT_lo[:, cols], tr_ps[:, 0:2 * w], hT_hi[:, cols].bitcast(F32),
                                        ALU.subtract).then_inc(hT_lo_ready, 1)

            def rest_of_agg(n, par, b):
                w = width(b)
                dve.wait_ge(agg_hi_ready, n + 1)
                split = lambda t: t.rearrange("f (j p) -> f j p", j=2)
                nc.vector.tensor_tensor(split(agg_lo[:, par, 0:2 * w]),
                                        aggT[:, bass.ds(b * BLOCK, 2 * w)].rearrange("f (p j) -> f j p", j=2),
                                        split(agg_hi[:, par, 0:2 * w].bitcast(F32)), ALU.subtract).then_inc(agg_lo_ready, 1)

            def prepare(c, s, par, q, k):
                if plain(par, k) or k == POOLED:
                    build(c, par, k)
                    return
                landed(dve, s, par, q, [k0 for k0, _ in PARTS if k0 <= k][-1])
                landed(dve, s, par, q, k)
                take_apart(nc.vector, dve, k, par * SC + k, apart_before(par, q, k), rem_ready, low_ready,
                           between=lambda: build(c, par, k))

            def add_chunk(c, base, slot, first=False):
                dve.wait_ge(chunk_summed, c + 1)
                if not first:
                    dve.wait_ge(agg_added, c)
                win = aggT[:, bass.ds(base, W)]
                nc.vector.tensor_tensor(win, chunk_ps[BANK[slot]][:, 0:W], win, ALU.add).then_inc(agg_added, 1)

            def step(s, par, q):
                last = is_last(s)
                _, bases = nc.values_load_multi_w_load_instructions(
                    base_tab[0:1, bass.ds(s, 1), :].rearrange("a s k -> a (s k)"), engines=[dve.engine], min_val=0,
                    max_val=N - 1, skip_runtime_bounds_check_because="clamped when written")
                for k in range(LASTC if last else SC):
                    c = s * SC + k
                    if k + LEAD < SC and (not last or k + LEAD < LASTC):
                        prepare(c + LEAD, s, par, q, k + LEAD)
                    elif not last and not (is_last(s + 1) and k + LEAD - SC >= LASTC):
                        prepare(c + LEAD, s + 1, 1 - par, q + par, k + LEAD - SC)
                    add_chunk(c, bases[k], par * SC + k, first=isinstance(c, int) and c == 0)
                    if k == 3:
                        rest_of_h(s)
                    if k == 2 and (not isinstance(s, int) or s >= 1):
                        rest_of_agg(s - 1, 1 - par, s - 1)

            def turned(half, done=None):
                if half == 0:
                    nc.vector.tensor_copy(relT[:, 0:P, 0:4].rearrange("p c g -> p g c"),
                                          hid_ps[0][:, :].rearrange("p (g c) -> p g c", c=P))
                    ins = nc.vector.tensor_copy(relT[:, 0:P, 4], hid_ps[1][:, 0:P])
                else:
                    ins = nc.vector.tensor_copy(relT[:, P:NCH, :].rearrange("p c g -> p g c"),
                                                out_ps[:, 0:G * CB].rearrange("p (g c) -> p g c", c=CB))
                ins.then_inc(done, 1)

            nc.vector.memset(base_tab[:, :, :], 0)
            nc.vector.memset(aggT[:, 0:HALF_AGG], 0.0).then_inc(agg_cleared, 1)
            halves = ((dstA, colA, relA), (dstB, colB, relB))
            for i, (d, col, rel) in enumerate(halves):
                dve.wait_ge(dst_landed[i], 16 * (i + 1))
                link(nc.vector.tensor_reduce(col[:, 0:1], d[:, :], AX_X, ALU.min))
                nc.vector.tensor_scalar(rel[:, :], d[:, :], col[:, 0:1], None, ALU.subtract).then_inc(rel_ready, 1)
            dve.wait_ge(rel_turned, 1)
            turned(0, rel_copied)
            dve.wait_ge(rel_copied, 1)
            dve.wait_ge(iota_ready, 2)
            build(0, 0, 0)
            link(nc.vector.tensor_copy(relT_h[:, 0:P, :], relT[:, 0:P, :]))
            for c in range(1, LEAD):
                prepare(c, 0, 0, 0, c)
            dve.wait_ge(columns_turned, 1)
            nc.vector.tensor_scalar(base_tab[:, 0:STEPS - 1, 0:SC],
                                    bases_ps[0:1, 0:(STEPS - 1) * SC].rearrange("a (s k) -> a s k", k=SC), 0.0,
                                    float(N - 1), ALU.max, ALU.min)
            nc.vector.tensor_scalar(base_tab[:, STEPS - 1, 0:LASTC], bases_ps[0:1, (STEPS - 1) * SC:NCH], 0.0,
                                    float(N - 1), ALU.max, ALU.min).then_inc(bases_ready, 1)
            dve.wait_ge(bases_ready, 1)
            dve.wait_ge(agg_cleared, 2)
            step(0, 0, 0)

            dve.wait_ge(rel_turned, 2)
            turned(1, rel_copied)
            dve.wait_ge(rel_copied, 2)
            nc.vector.tensor_copy(relT_h[:, P:NCH, :], relT[:, P:NCH, :])
            step(1, 1, 0)
            for s in range(2, 5):
                step(s, s % 2, s // 2)
            with dve.Fori(2, (STEPS - 4) // 2) as m:
                step(2 * m + 1, 1, m)
                step(2 * m + 2, 0, m + 1)
            for s in range(STEPS - 3, STEPS):
                step(s, s % 2, s // 2)
            rest_of_agg(NB - 2, (NB - 2) % 2, NB - 2)
            dve.wait_ge(constants_ready, 2)
            for (_, col, rel), lim in zip(halves, (limit[:, 0:1], limit[0:CB, 1:2])):
                nc.vector.tensor_reduce(col[:, 1:2], rel[:, :], AX_X, ALU.max)
                link(nc.vector.scalar_tensor_tensor(col[:, 3:4], col[:, 0:1], float(-SC), lim, ALU.mult, ALU.add))
                link(nc.vector.tensor_scalar(col[:, 2:3], col[:, 1:2], float(-(W - 1)), None, ALU.add))
                nc.vector.tensor_tensor(col[:, 4:5], col[:, 2:3], col[:, 3:4], ALU.max).then_inc(overrun_ready, 1)
            rest_of_h(NB - 1)
            rest_of_agg(NB - 1, (NB - 1) % 2, NB - 1)
            dve.wait_ge(columns_turned, 3)
            link(nc.vector.tensor_reduce(over[:, :], bases_ps[0:1, 0:NCH], AX_X, ALU.max))
            nc.vector.tensor_scalar(flag[:, :], over[:, :], 0.0, None, ALU.is_gt).then_inc(flag_ready, 1)

            dve.wait_ge(flag_ready, 1)
            again = dve.value_load(flag[0:1, 0:1], min_val=0, max_val=1)
            with dve.If(again > 0):
                for col, rel, d in ((colA, relA, dstA), (colB, relB, dstB)):
                    hot = edges[0:rel.shape[0], 1, 0:CHUNK]
                    nc.vector.tensor_scalar(hot, rel[:, :], float(W), None, ALU.is_ge).then_inc(wide_dst_ready, 1)
                    nc.vector.tensor_scalar(col[:, 5:6], col[:, 0:1], 1.0, None, ALU.add).then_inc(wide_dst_ready, 1)
                    dve.wait_ge(wide_dst_ready, 2 if rel is relA else 4)
                    nc.vector.scalar_tensor_tensor(rel[:, :], rel[:, :], col[:, 5:6], hot, ALU.add,
                                                   ALU.mult).then_inc(wide_rel_ready, 1)
                    dve.wait_ge(wide_rel_ready, 1 if rel is relA else 2)
                dve.wait_ge(wide_summed, 1)
                turned(0, rel_copied)
                turned(1, wide_added)

                def wide(c):
                    with dve.Fori(0, NWIDE) as j:
                        n = c * NWIDE + j
                        dve.wait_ge(wide_added, n + 1)
                        nc.vector.tensor_scalar(wide_dst[:, :], at(relT, c).rearrange("p c g -> p (c g)"),
                                                wide_base[:, bass.ds(j, 1)], None, ALU.subtract).then_inc(wide_dst_ready, 1)
                        dve.wait_ge(wide_dst_ready, 4 + n + 1)
                        nc.vector.tensor_tensor(wide_hot[:, :, :], wide_dst[:, :].unsqueeze(2).to_broadcast([P, G, WIDE]),
                                                iota[:, :].unsqueeze(1).to_broadcast([P, G, WIDE]),
                                                ALU.is_equal).then_inc(wide_hot_ready, 1)
                        dve.wait_ge(wide_summed, n + 2)
                        win = aggT[:, bass.ds(j * WIDE, WIDE)]
                        nc.vector.tensor_tensor(win, chunk_ps[0][:, :], win, ALU.add).then_inc(wide_added, 1)

                wide_base = xn[:, 0, 0, 0:NWIDE]
                for j in range(NWIDE):
                    nc.vector.memset(wide_base[:, j:j + 1], float(j * WIDE + 1)).then_inc(wide_rel_ready, 1)
                dve.wait_ge(wide_rel_ready, 2 + NWIDE)
                with dve.Fori(0, NCH) as c:
                    wide(c)

                with dve.Fori(0, (NB - 1) // 2) as i:
                    rest_of_agg(NB + 2 * i, 1, 2 * i)
                    rest_of_agg(NB + 2 * i + 1, 0, 2 * i + 1)
                rest_of_agg(2 * NB - 1, 1, NB - 1)

        @block.tensor
        def _(pe):
            def turn_rel(half, done):
                for g in range(G):
                    if half == 0:
                        o = hid_ps[0][:, g * P:(g + 1) * P] if g < 4 else hid_ps[1][:, 0:P]
                        ins = nc.tensor.transpose(o, relA[:, g:CHUNK:G], ident[:, :])
                    else:
                        ins = nc.tensor.transpose(out_ps[:, g * CB:(g + 1) * CB], relB[:, g:CHUNK:G],
                                                  ident[0:CB, 0:CB])
                ins.then_inc(done, 1)

            def turn_columns(o, i):
                nc.tensor.transpose(o[0:1, 0:P], colA[:, i:i + 1], ident[:, :])
                return nc.tensor.transpose(o[0:1, P:NCH], colB[:, i:i + 1], ident[0:CB, 0:CB])

            def sum_chunk(c, s, par, q, k):
                kp = KREST if isinstance(c, int) and c == NCH - 1 else P
                slot = par * SC + k
                landed(pe, s, par, q, k)
                pe.wait_ge(onehot_ready, c + 1)
                if isinstance(c, int) and c == 3:
                    pe.wait_ge(bases_ready, 1)
                if not isinstance(c, int) or c >= SINCE[slot]:
                    pe.wait_ge(agg_added, c - SINCE[slot] + 1)
                sums_ps = chunk_ps[BANK[slot]][:, 0:W]
                if plain(par, k):
                    for g in range(G):
                        ins = nc.tensor.matmul(sums_ps, edges[0:kp, slot, g * F:(g + 1) * F],
                                               onehot[0:kp, PLAIN.index(k), g, :], start=(g == 0), stop=(g == G - 1))
                else:
                    i = HALVED.index(k)
                    if k == POOLED:
                        pe.wait_ge(pool_low_ready, s + 1)
                    else:
                        pe.wait_ge(low_ready, apart_before(par, q, k) + 1)
                    high, middle = upper(edges[:, slot, :]), upper(rem[:, i, :])
                    for g in range(G):
                        hot, cols = onehot_h[0:kp, i, :, g], slice(g * F, (g + 1) * F)
                        nc.tensor.matmul(sums_ps, high[0:kp, cols], hot, start=(g == 0), stop=False)
                        nc.tensor.matmul(sums_ps, middle[0:kp, cols], hot, start=False, stop=False)
                        ins = nc.tensor.matmul(sums_ps, low[0:kp, i, cols], hot, start=False, stop=(g == G - 1))
                ins.then_inc(chunk_summed, 1)

            def turn_x(b, par, first=False):
                w = width(b)
                pe.wait_ge(xn_ready, b + 1)
                if not first:
                    pe.wait_ge(hT_lo_ready, b)
                for j in range(2):
                    ins = nc.tensor.transpose(tr_ps[:, j * w:(j + 1) * w], xn[0:w, par, j, :], ident[0:w, 0:w])
                ins.then_inc(h_turned, 1)

            def layer1(n, par, b, tiles=range(HT)):
                w = width(b)
                pe.wait_ge(agg_lo_ready, n + 1)
                for t in tiles:
                    if t % 2 == 0:
                        pe.wait_ge(hidden_ready, n * HT + t + 2)
                    o = hid_ps[t // 2][:, (t % 2) * 2 * w:(t % 2 + 1) * 2 * w]
                    cols = slice(t * P, (t + 1) * P)
                    here = bass.ds(b * BLOCK, 2 * w)
                    products = ((w1_hi, 1, hT_hi[:, here]), (w1_hi, 1, hT_lo[:, here]), (w1_lo, 1, hT_hi[:, here]),
                                (w1_hi, 0, agg_hi[:, par, 0:2 * w]), (w1_hi, 0, agg_lo[:, par, 0:2 * w]),
                                (w1_lo, 0, agg_hi[:, par, 0:2 * w]))
                    for i, (wt, half, v) in enumerate(products):
                        ins = nc.tensor.matmul(o, wt[:, half, cols], v, start=(i == 0), stop=(i == 5))
                    if t % 2 == 1:
                        ins.then_inc(hidden_summed, 1)

            def layer2(n, par, b, slots=range(2)):
                w = width(b)
                if not isinstance(n, int) or n > 0:
                    pe.wait_ge(out_copied, n)
                for j in slots:
                    for t in range(HT):
                        if j == 0:
                            pe.wait_ge(hidden_ready, (n + 1) * HT + t + 1)
                        ins = nc.tensor.matmul(out_ps[0:w, j * F:(j + 1) * F], hidden[par][:, t, j * w:(j + 1) * w],
                                               w2[:, t, :], start=(t == 0), stop=(t == HT - 1))
                if j == 1:
                    ins.then_inc(out_summed, 1)

            def step(s, par, q):
                for k in range(LASTC if is_last(s) else SC):
                    sum_chunk(s * SC + k, s, par, q, k)
                    if k == 0:
                        turn_x(s, par, first=isinstance(s, int) and s == 0)
                    if not isinstance(s, int) or s >= 2:
                        if k == 1:
                            layer2(s - 2, par, s - 2, slots=[0])
                        if k == 2:
                            layer2(s - 2, par, s - 2, slots=[1])
                    if not isinstance(s, int) or s >= 1:
                        if k == 5:
                            pe.wait_ge(hT_lo_ready, s)
                            layer1(s - 1, 1 - par, s - 1, tiles=[0, 1])
                        if k == (min(6, LASTC - 1) if is_last(s) else 6):
                            layer1(s - 1, 1 - par, s - 1, tiles=[2, 3])

            pe.wait_ge(constants_ready, 1)
            pe.wait_ge(rel_ready, 1)
            turn_rel(0, rel_turned)
            pe.wait_ge(rel_ready, 2)
            turn_columns(bases_ps, 0).then_inc(columns_turned, 1)
            turn_rel(1, rel_turned)
            step(0, 0, 0)
            pe.wait_ge(weights_landed, 64)
            nc.tensor.transpose(hid_ps[0][:, 0:HT], b1_row[:, :], ident[0:HT, 0:HT]).then_inc(columns_turned, 1)
            pe.wait_ge(w1_ready, 1)
            step(1, 1, 0)
            pe.wait_ge(rel_copied, 2)
            step(2, 0, 1)
            with pe.Fori(1, (STEPS - 2) // 2) as m:
                step(2 * m + 1, 1, m)
                step(2 * m + 2, 0, m + 1)
            step(STEPS - 1, 1, (STEPS - 1) // 2)
            turn_x(NB - 1, 0)
            pe.wait_ge(hT_lo_ready, NB - 1)
            layer1(NB - 2, 1, NB - 2)
            layer2(NB - 3, 0, NB - 3)
            pe.wait_ge(hT_lo_ready, NB)
            layer1(NB - 1, 0, NB - 1)
            pe.wait_ge(overrun_ready, 2)
            turn_columns(bases_ps, 4).then_inc(columns_turned, 1)
            for b in (NB - 2, NB - 1):
                layer2(b, b % 2, b)

            pe.wait_ge(flag_ready, 1)
            again = pe.value_load(flag[0:1, 0:1], min_val=0, max_val=1)
            with pe.If(again > 0):
                pe.wait_ge(wide_rel_ready, 2)
                pe.wait_ge(out_copied, NB)
                turn_rel(0, rel_turned)
                turn_rel(1, wide_summed)

                def wide(c, kp):
                    with pe.Fori(0, NWIDE) as j:
                        n = c * NWIDE + j
                        pe.wait_ge(wide_landed, 16 * (c + 1))
                        pe.wait_ge(wide_hot_ready, n + 1)
                        for g in range(G):
                            ins = nc.tensor.matmul(chunk_ps[0][:, :], edges[0:kp, 0, g * F:(g + 1) * F],
                                                   wide_hot[0:kp, g, :], start=(g == 0), stop=(g == G - 1))
                        ins.then_inc(wide_summed, 1)

                with pe.Fori(0, FULL) as c:
                    wide(c, P)
                wide(FULL, KREST)

                def again_block(n, par, b):
                    layer1(n, par, b)
                    layer2(n, par, b)

                with pe.Fori(0, (NB - 1) // 2) as i:
                    again_block(NB + 2 * i, 1, 2 * i)
                    again_block(NB + 2 * i + 1, 0, 2 * i + 1)
                again_block(2 * NB - 1, 1, NB - 1)


_INS = ["x", "dst", "edge_attr_128", "L0_gnn_W1", "L0_gnn_b1", "L0_gnn_W2", "L0_gnn_b2"]


def kernel(**inputs):
    import numpy as _np
    import concourse.bacc as _bacc
    from concourse import mybir as _mybir
    from concourse.bass_utils import run_bass_kernel_spmd as _run

    nc = _bacc.Bacc("TRN2", target_bir_lowering=False, num_devices=1)
    arrays, args = {}, []
    for name in _INS:
        a = _np.ascontiguousarray(inputs[name])
        arrays[f"in_{name}"] = a
        args.append(nc.dram_tensor(f"in_{name}", a.shape, _mybir.dt.from_np(a.dtype), kind="ExternalInput").ap())
    out = nc.dram_tensor("out_rows", inputs["x"].shape, F32, kind="ExternalOutput").ap()
    graph_layer(nc, *args, out)
    r = _run(nc, [arrays], core_ids=[0])
    return r.results[0]["out_rows"]
```
